# Optimizing a Trainium2 kernel written in Bass

```python
import numpy as np
import jax
import jax.numpy as jnp

def _softmax(x, axis=-1):
    return jax.nn.softmax(x, axis=axis)

def _gelu(x):
    return jax.nn.gelu(x, approximate=True)

def _silu(x):
    return jax.nn.silu(x)

def _sigmoid(x):
    return jax.nn.sigmoid(x)

def _layernorm(x, axis=-1, eps=1e-05):
    m = jnp.mean(x, axis=axis, keepdims=True)
    v = jnp.var(x, axis=axis, keepdims=True)
    return (x - m) / jnp.sqrt(v + eps)

def _scatter_add(tgt, idx, src, axis=0):
    return tgt.at[idx].add(src)

def _segment_sum(src, seg, n):
    return jax.ops.segment_sum(src, seg, n)
kernel_name = 'mk_cond_resid_d2_seqx_r2_781234'

def setup_inputs(seed: int=0):
    np.random.seed(seed)
    _w = jnp.asarray

    def _rec_inputs():
        import jax
        import jax.numpy as jnp
        _rk = jax.random.key(seed)
        x = -0.0002928 + 1 * jax.random.normal(jax.random.fold_in(_rk, 1), (64, 128, 512), jnp.float32)
        _lenS = 128 - jax.random.randint(jax.random.fold_in(_rk, 7), (64,), 0, max(1, 128 // 4) + 1, jnp.int32)
        _lenS2 = 128 - jax.random.randint(jax.random.fold_in(_rk, 8), (64,), 0, max(1, 128 // 4) + 1, jnp.int32)
        fside_16xSxS_0 = -5.72187e-05 + 0.999849 * jax.random.normal(jax.random.fold_in(_rk, 11), (16, 128, 128), jnp.float32)
        cond_64 = -0.0265395 + 0.99382 * jax.random.normal(jax.random.fold_in(_rk, 13), (64, 64), jnp.float32)
        _validS = jnp.arange(128)[None, :] < _lenS[:, None]
        _validS2 = jnp.arange(128)[None, :] < _lenS2[:, None]
        _causal = jnp.tril(jnp.ones((128, 128), dtype=bool))
        mask_BxS_bk0 = jnp.logical_not(jnp.broadcast_to(_validS[:, :], (64, 128)))
        mask_BxS_bf1 = jnp.ones((64, 128), dtype=bool)
        return (x, fside_16xSxS_0, cond_64, mask_BxS_bk0, mask_BxS_bf1)
    x, fside_16xSxS_0, cond_64, mask_BxS_bk0, mask_BxS_bf1 = _rec_inputs()

    def _L0_cond_setup():
        import jax, jax.numpy as jnp
        import numpy as np
        B, N, DIM, H, DH = (2, 1024, 512, 16, 64)
        INNER = H * DH
        EPS = 1e-05

        def layernorm(x, g):
            mean = jnp.mean(x, axis=-1, keepdims=True)
            var = jnp.var(x, axis=-1, keepdims=True)
            return (x - mean) * jax.lax.rsqrt(var + EPS) * g
        key = jax.random.key(seed)
        ks = jax.random.split(key, 10)
        x = jax.random.normal(ks[0], (B, N, DIM), dtype=jnp.float32)
        attn_bias = jax.random.normal(ks[1], (H, N, N), dtype=jnp.float32)
        mask = jax.random.randint(ks[2], (B, N), 0, 2).astype(bool)
        g_in = jnp.ones((DIM,), dtype=jnp.float32)
        null_attn_bias = jax.random.normal(ks[3], (H,), dtype=jnp.float32)
        null_kv = jax.random.normal(ks[4], (2, DH), dtype=jnp.float32)
        Wq = jax.random.normal(ks[5], (DIM, INNER), dtype=jnp.float32) * 0.02
        Wkv = jax.random.normal(ks[6], (DIM, 2 * DH), dtype=jnp.float32) * 0.02
        Wo = jax.random.normal(ks[7], (INNER, DIM), dtype=jnp.float32) * 0.02
        g_out = jnp.ones((DIM,), dtype=jnp.float32)
        return {'x': x, 'attn_bias': attn_bias, 'mask': mask, 'g_in': g_in, 'null_attn_bias': null_attn_bias, 'null_kv': null_kv, 'Wq': Wq, 'Wkv': Wkv, 'Wo': Wo, 'g_out': g_out}
    _L0_cond_all = _L0_cond_setup()
    _L0_cond_in = {k: v for k, v in _L0_cond_all.items() if k in ('g_in', 'null_attn_bias', 'Wq', 'Wkv', 'Wo', 'g_out')}
    del _L0_cond_all

    def _L1_cond_setup():
        import jax, jax.numpy as jnp
        import numpy as np
        DIM = 512
        HEADS = 16
        DIM_HEAD = 64
        SCALE = 8.0

        def ln(x, g, eps=1e-05):
            mean = x.mean(axis=-1, keepdims=True)
            var = ((x - mean) ** 2).mean(axis=-1, keepdims=True)
            return (x - mean) * jax.lax.rsqrt(var + eps) * g

        def l2norm(t):
            n = jnp.maximum(jnp.linalg.norm(t, axis=-1, keepdims=True), 1e-12)
            return t / n

        def rel_pos_bias(n, w0, b0, g0, w1, b1, g1, w2, b2, dtype):
            pos = jnp.arange(-n + 1, n, dtype=dtype)[:, None]
            h = jax.nn.silu(ln(pos @ w0 + b0, g0))
            h = jax.nn.silu(ln(h @ w1 + b1, g1))
            h = h @ w2 + b2
            i = jnp.arange(n)
            idx = i[:, None] - i[None, :] + n - 1
            bias = h[idx]
            return jnp.transpose(bias, (2, 0, 1))
        key = jax.random.key(seed)
        ks = jax.random.split(key, 16)
        b, n = (2, 1024)
        inner = HEADS * DIM_HEAD
        s = 0.02
        return {'x': jax.random.normal(ks[0], (b, n, DIM), jnp.float32), 'mask': jnp.ones((b, n), dtype=bool), 'g_norm': jnp.ones((DIM,), jnp.float32), 'Wq': jax.random.normal(ks[1], (DIM, inner), jnp.float32) * s, 'Wkv': jax.random.normal(ks[2], (DIM, 2 * DIM_HEAD), jnp.float32) * s, 'q_scale': jnp.ones((DIM_HEAD,), jnp.float32), 'k_scale': jnp.ones((DIM_HEAD,), jnp.float32), 'null_kv': jax.random.normal(ks[3], (2, DIM_HEAD), jnp.float32), 'null_attn_bias': jax.random.normal(ks[4], (HEADS,), jnp.float32), 'w0': jax.random.normal(ks[5], (1, DIM), jnp.float32) * s, 'b0': jnp.zeros((DIM,), jnp.float32), 'g0': jnp.ones((DIM,), jnp.float32), 'w1': jax.random.normal(ks[6], (DIM, DIM), jnp.float32) * s, 'b1': jnp.zeros((DIM,), jnp.float32), 'g1': jnp.ones((DIM,), jnp.float32), 'w2': jax.random.normal(ks[7], (DIM, HEADS), jnp.float32) * s, 'b2': jnp.zeros((HEADS,), jnp.float32), 'Wout': jax.random.normal(ks[8], (inner, DIM), jnp.float32) * s, 'g_out': jnp.ones((DIM,), jnp.float32)}
    _L1_cond_all = _L1_cond_setup()
    _L1_cond_in = {k: v for k, v in _L1_cond_all.items() if k in ('g_norm', 'Wq', 'Wkv', 'q_scale', 'k_scale', 'null_attn_bias', 'w0', 'b0', 'g0', 'w1', 'b1', 'g1', 'w2', 'b2', 'Wout', 'g_out')}
    del _L1_cond_all
    return {'x': x, 'fside_16xSxS_0': fside_16xSxS_0, 'cond_64': cond_64, 'mask_BxS_bk0': mask_BxS_bk0, 'mask_BxS_bf1': mask_BxS_bf1, 'L0_cond_g_in': _L0_cond_in['g_in'], 'L0_cond_null_attn_bias': _L0_cond_in['null_attn_bias'], 'L0_cond_Wq': _L0_cond_in['Wq'], 'L0_cond_Wkv': _L0_cond_in['Wkv'], 'L0_cond_Wo': _L0_cond_in['Wo'], 'L0_cond_g_out': _L0_cond_in['g_out'], 'L1_cond_g_norm': _L1_cond_in['g_norm'], 'L1_cond_Wq': _L1_cond_in['Wq'], 'L1_cond_Wkv': _L1_cond_in['Wkv'], 'L1_cond_q_scale': _L1_cond_in['q_scale'], 'L1_cond_k_scale': _L1_cond_in['k_scale'], 'L1_cond_null_attn_bias': _L1_cond_in['null_attn_bias'], 'L1_cond_w0': _L1_cond_in['w0'], 'L1_cond_b0': _L1_cond_in['b0'], 'L1_cond_g0': _L1_cond_in['g0'], 'L1_cond_w1': _L1_cond_in['w1'], 'L1_cond_b1': _L1_cond_in['b1'], 'L1_cond_g1': _L1_cond_in['g1'], 'L1_cond_w2': _L1_cond_in['w2'], 'L1_cond_b2': _L1_cond_in['b2'], 'L1_cond_Wout': _L1_cond_in['Wout'], 'L1_cond_g_out': _L1_cond_in['g_out']}

def reference(x, fside_16xSxS_0, cond_64, mask_BxS_bk0, mask_BxS_bf1, L0_cond_g_in, L0_cond_null_attn_bias, L0_cond_Wq, L0_cond_Wkv, L0_cond_Wo, L0_cond_g_out, L1_cond_g_norm, L1_cond_Wq, L1_cond_Wkv, L1_cond_q_scale, L1_cond_k_scale, L1_cond_null_attn_bias, L1_cond_w0, L1_cond_b0, L1_cond_g0, L1_cond_w1, L1_cond_b1, L1_cond_g1, L1_cond_w2, L1_cond_b2, L1_cond_Wout, L1_cond_g_out):
    import jax
    import jax.numpy as jnp

    def _L0_cond_ref(x, attn_bias, mask, g_in, null_attn_bias, null_kv, Wq, Wkv, Wo, g_out):
        import jax, jax.numpy as jnp
        import numpy as np
        B, N, DIM, H, DH = (2, 1024, 512, 16, 64)
        INNER = H * DH
        EPS = 1e-05

        def layernorm(x, g):
            mean = jnp.mean(x, axis=-1, keepdims=True)
            var = jnp.var(x, axis=-1, keepdims=True)
            return (x - mean) * jax.lax.rsqrt(var + EPS) * g
        b, n, _ = x.shape
        scale = DH ** (-0.5)
        xn = layernorm(x, g_in)
        q = (xn @ Wq).reshape(b, n, H, DH).transpose(0, 2, 1, 3) * scale
        kv = xn @ Wkv
        k, v = (kv[..., :DH], kv[..., DH:])
        nk = jnp.broadcast_to(null_kv[0], (b, 1, DH))
        nv = jnp.broadcast_to(null_kv[1], (b, 1, DH))
        k = jnp.concatenate([nk, k], axis=1)
        v = jnp.concatenate([nv, v], axis=1)
        sim = jnp.einsum('bhid,bjd->bhij', q, k)
        null_col = jnp.broadcast_to(null_attn_bias[:, None, None], (H, n, 1))
        bias = jnp.concatenate([null_col, attn_bias], axis=-1)
        sim = sim + bias
        neg = -jnp.finfo(sim.dtype).max
        j = n + 1
        causal_mask = jnp.triu(jnp.ones((n, j), dtype=bool), k=j - n + 1)
        sim = jnp.where(causal_mask, neg, sim)
        mask_p = jnp.pad(mask, ((0, 0), (1, 0)), constant_values=True)
        sim = jnp.where(mask_p[:, None, None, :], sim, neg)
        attn = jax.nn.softmax(sim, axis=-1)
        out = jnp.einsum('bhij,bjd->bhid', attn, v)
        out = out.transpose(0, 2, 1, 3).reshape(b, n, INNER)
        out = out @ Wo
        return layernorm(out, g_out)

    def _L1_cond_ref(x, mask, g_norm, Wq, Wkv, q_scale, k_scale, null_kv, null_attn_bias, w0, b0, g0, w1, b1, g1, w2, b2, Wout, g_out):
        import jax, jax.numpy as jnp
        import numpy as np
        DIM = 512
        HEADS = 16
        DIM_HEAD = 64
        SCALE = 8.0

        def ln(x, g, eps=1e-05):
            mean = x.mean(axis=-1, keepdims=True)
            var = ((x - mean) ** 2).mean(axis=-1, keepdims=True)
            return (x - mean) * jax.lax.rsqrt(var + eps) * g

        def l2norm(t):
            n = jnp.maximum(jnp.linalg.norm(t, axis=-1, keepdims=True), 1e-12)
            return t / n

        def rel_pos_bias(n, w0, b0, g0, w1, b1, g1, w2, b2, dtype):
            pos = jnp.arange(-n + 1, n, dtype=dtype)[:, None]
            h = jax.nn.silu(ln(pos @ w0 + b0, g0))
            h = jax.nn.silu(ln(h @ w1 + b1, g1))
            h = h @ w2 + b2
            i = jnp.arange(n)
            idx = i[:, None] - i[None, :] + n - 1
            bias = h[idx]
            return jnp.transpose(bias, (2, 0, 1))
        b, n, _ = x.shape
        xn = ln(x, g_norm)
        q = (xn @ Wq).reshape(b, n, HEADS, DIM_HEAD).transpose(0, 2, 1, 3)
        kv = xn @ Wkv
        k, v = (kv[..., :DIM_HEAD], kv[..., DIM_HEAD:])
        nk = jnp.broadcast_to(null_kv[0], (b, 1, DIM_HEAD))
        nv = jnp.broadcast_to(null_kv[1], (b, 1, DIM_HEAD))
        k = jnp.concatenate([nk, k], axis=1)
        v = jnp.concatenate([nv, v], axis=1)
        q = l2norm(q) * q_scale
        k = l2norm(k) * k_scale
        sim = jnp.einsum('bhid,bjd->bhij', q, k) * SCALE
        bias = rel_pos_bias(n, w0, b0, g0, w1, b1, g1, w2, b2, q.dtype)
        null_bias = jnp.broadcast_to(null_attn_bias[:, None, None], (HEADS, n, 1))
        attn_bias = jnp.concatenate([null_bias, bias], axis=-1)
        sim = sim + attn_bias
        neg = -jnp.finfo(sim.dtype).max
        causal = jnp.triu(jnp.ones((n, n + 1), dtype=bool), k=2)
        sim = jnp.where(causal, neg, sim)
        m = jnp.pad(mask, ((0, 0), (1, 0)), constant_values=True)[:, None, None, :]
        sim = jnp.where(m, sim, neg)
        attn = jax.nn.softmax(sim, axis=-1)
        out = jnp.einsum('bhij,bjd->bhid', attn, v)
        out = out.transpose(0, 2, 1, 3).reshape(b, n, HEADS * DIM_HEAD)
        return ln(out @ Wout, g_out)
    x = x + _L0_cond_ref(x, fside_16xSxS_0, mask_BxS_bk0, L0_cond_g_in, L0_cond_null_attn_bias, cond_64, L0_cond_Wq, L0_cond_Wkv, L0_cond_Wo, L0_cond_g_out)
    x = x + _L1_cond_ref(x, mask_BxS_bf1, L1_cond_g_norm, L1_cond_Wq, L1_cond_Wkv, L1_cond_q_scale, L1_cond_k_scale, cond_64, L1_cond_null_attn_bias, L1_cond_w0, L1_cond_b0, L1_cond_g0, L1_cond_w1, L1_cond_b1, L1_cond_g1, L1_cond_w2, L1_cond_b2, L1_cond_Wout, L1_cond_g_out)
    return x

_drawn_inputs = setup_inputs


def setup_inputs(seed=0):
    import zlib

    import numpy as np

    out = dict(_drawn_inputs(seed))
    spreads = {'L0_cond_g_in': (1.0, 0.2),
     'L0_cond_g_out': (1.0, 0.2),
     'L1_cond_g_norm': (1.0, 0.2),
     'L1_cond_q_scale': (1.0, 0.578),
     'L1_cond_k_scale': (1.0, 0.2),
     'L1_cond_b0': (0.0, 0.303),
     'L1_cond_g0': (1.0, 0.6),
     'L1_cond_b1': (0.0, 0.8),
     'L1_cond_g1': (1.0, 0.6),
     'L1_cond_b2': (0.0, 0.8),
     'L1_cond_g_out': (1.0, 0.2)}
    factors = {'L1_cond_w0': 2.882}
    for name, (base, spread) in spreads.items():
        noise = np.random.default_rng([zlib.crc32(name.encode()), seed]).standard_normal(out[name].shape)
        drawn = base * np.exp(spread * noise) if base else spread * noise
        out[name] = jnp.asarray(drawn.astype(out[name].dtype))
    for name, factor in factors.items():
        out[name] = (out[name] * factor).astype(out[name].dtype)
    return out
```

```python
from contextlib import ExitStack

import concourse.bass as bass
from concourse import mybir

F32 = mybir.dt.float32
F32R = mybir.dt.float32r
U8 = mybir.dt.uint8
ALU = mybir.AluOpType
ACT = mybir.ActivationFunctionType
AX = mybir.AxisListType

P = 128
EPS = 1e-5
NEG = -1e38
NORM_FLOOR = 1e-24
NORM_SCALE = 2.0 ** 16
LN_NORM_ROOT = 8 * 0.6931471805599453


class Unit:

    def __init__(self, layer, batch, done, prev, same, sdone):
        self.layer, self.batch, self.done, self.prev, self.same, self.sdone = layer, batch, done, prev, same, sdone


def static_unit(layer, batch, nb):
    if layer == 0:
        u = 0 if batch == 0 else 2 * batch - 1
    else:
        u = 2 * batch + 2 if batch < nb - 1 else 2 * nb - 1
    return Unit(layer, batch, u + 1, u, batch, batch + 1)


def wait(eng, sem, value):
    if isinstance(value, int) and value <= 0:
        return
    eng.wait_ge(sem, value)


def wait_apart(eng, sem, value, passed):
    if not isinstance(value, int):
        eng.wait_ge(sem, value)
        eng.sem_inc(passed, 1)
    else:
        wait(eng, sem, value)


def run_units(eng, body, nb):
    A = lambda a: static_unit(0, a, nb)
    B = lambda b: static_unit(1, b, nb)
    body(A(0), None, None, None, True)
    body(A(1), A(0), None, B(0), True)
    body(A(2), A(1), B(0), B(1), True)
    with eng.Fori(3, nb - 1) as i:
        v = {0: i}
        for k in range(-3, 2):
            v[10 + k] = eng.snap(i * 2 + k)
        im1 = eng.snap(i - 1)
        im2 = eng.snap(i - 2)
        ip1 = eng.snap(i + 1)
        a = Unit(0, i, v[10], v[9], i, ip1)
        ap = Unit(0, im1, v[8], v[7], im1, i)
        bo = Unit(1, im2, v[9], v[8], im2, im1)
        bn = Unit(1, im1, v[11], v[10], im1, i)
        body(a, ap, bo, bn, True)
    body(A(nb - 1), A(nb - 2), B(nb - 3), B(nb - 2), False)
    body(None, A(nb - 1), B(nb - 2), B(nb - 1), False)
    body(None, None, B(nb - 1), None, False)


def build(nc, x, bias0, null_kv, keep0, keep1, L0, L1, out):
    NB, S, D = x.shape
    H = bias0.shape[0]
    INNER = L0["Wq"].shape[1]
    DH = INNER // H
    KC = D // P
    PAIRS = H // 2
    COLS = INNER + 2 * DH + H
    HG = 6
    QB = [(0, HG * DH), (HG * DH, 2 * HG * DH), (2 * HG * DH, COLS)]
    QH = [(0, HG), (HG, 2 * HG), (2 * HG, H)]
    Q2 = 2 * HG * DH
    KO, VO, SO = INNER - Q2, INNER - Q2 + DH, INNER - Q2 + 2 * DH
    CH = 4
    NCH = H // CH
    assert S == P and DH == 64 and COLS - Q2 <= 512 and D == 512

    ctx = ExitStack()
    with ctx:
        def sb(name, shape, dt=F32, where=ctx):
            return where.enter_context(nc.sbuf_tensor(name, shape, dt))

        def sem(name):
            return ctx.enter_context(nc.semaphore(name))

        psum = ctx.enter_context(nc.psum_tensor("psum", [P, 8, 512], F32))
        Q = [psum[:, b, :] for b in range(3)]
        SP = [psum[:, 3 + b, :] for b in range(2)]
        O = [psum[:, 5 + b, :] for b in range(2)]
        Y = psum[:, 7, :]

        w_hi = [sb(f"w_hi{n}", [P, KC, COLS], F32R) for n in range(2)]
        w_lo = [sb(f"w_lo{n}", [P, KC, COLS], F32R) for n in range(2)]
        wo_hi = [sb(f"wo_hi{n}", [P, PAIRS, D], F32R) for n in range(2)]
        wo_lo = [sb(f"wo_lo{n}", [P, PAIRS, D], F32R) for n in range(2)]
        bias = [sb(f"bias{n}", [P, H, S]) for n in range(2)]
        g_out = [sb(f"g_out{n}", [P, D]) for n in range(2)]
        null_bias = [sb(f"null_bias{n}", [P, H]) for n in range(2)]
        k_scale = [sb(f"k_scale{n}", [P, 1]) for n in range(2)]
        null_v = sb("null_v", [P, DH])
        null_v_col = sb("null_v_col", [P, 1])
        ident = sb("ident", [P, P])
        eps_col = sb("eps_col", [P, 1])
        root_col = sb("root_col", [P, 1])
        k_diag = sb("k_diag", [P, 2 * S])

        setup(nc, ctx, null_kv, bias0, L0, L1, dict(
            KC=KC, COLS=COLS, INNER=INNER, DH=DH, H=H, D=D, S=S, PAIRS=PAIRS, w_hi=w_hi, w_lo=w_lo, wo_hi=wo_hi, wo_lo=wo_lo,
            bias=bias, g_out=g_out, null_bias=null_bias, k_scale=k_scale, null_v=null_v, null_v_col=null_v_col, ident=ident,
            eps_col=eps_col, root_col=root_col, k_diag=k_diag, psum=psum))

        xa = sb("xa", [P, D])
        x_res = sb("x_res", [P, D])
        x1 = sb("x1", [P, D])
        x1_res = sb("x1_res", [P, D])
        x_out = sb("x_out", [P, D])
        xn = sb("xn", [P, D])
        x_hi = sb("x_hi", [P, D], F32R)
        x_lo = sb("x_lo", [P, D], F32R)
        q_sb = sb("q_sb", [P, INNER])
        q_t = sb("q_t", [P, INNER])
        k_dup = sb("k_dup", [P, 2, DH])
        v_diff = [sb(f"v_diff{n}", [P, DH]) for n in range(2)]
        s0 = [sb(f"s0_{n}", [P, H]) for n in range(2)]
        masked_bias = sb("masked_bias", [P, H, S])
        pad_neg = sb("pad_neg", [P, S])
        keep = [sb(f"keep{n}", [P, S], U8) for n in range(2)]
        probs = sb("probs", [P, H, S + 1])
        o_hi = sb("o_hi", [P, PAIRS * P], F32R)
        o_lo = sb("o_lo", [P, PAIRS * P], F32R)
        bn_in = sb("bn_in", [P, 6])
        mv_in = sb("mv_in", [P, 2])
        rstd_in = sb("rstd_in", [P, 1])
        ln_in = sb("ln_in", [P, 1])
        bn_out = sb("bn_out", [P, 6])
        mv_out = sb("mv_out", [P, 2])
        rstd_out = sb("rstd_out", [P, 1])
        ln_out = sb("ln_out", [P, 1])
        norm_sq = sb("norm_sq", [P, H + 1])
        norm_ln = sb("norm_ln", [P, H + 1])
        norm_inv = sb("norm_inv", [P, H + 1])
        neg_max = sb("neg_max", [P, H])
        den = sb("den", [P, H])
        den_inv = sb("den_inv", [P, H])

        xa_loaded, x_res_loaded = sem("xa_loaded"), sem("x_res_loaded")
        keep_loaded = [sem(f"keep_loaded{n}") for n in range(2)]
        x1_copied, out_stored = sem("x1_copied"), sem("out_stored")
        bn_in_done, mv_in_done, ln_in_done, rstd_in_done = (sem(n) for n in ("bn_in_done", "mv_in_done", "ln_in_done", "rstd_in_done"))
        xn_done, xt_done, x_hi_done, x_lo_done = (sem(n) for n in ("xn_done", "xt_done", "x_hi_done", "x_lo_done"))
        proj_done = [sem(f"proj_done{n}") for n in range(3)]
        q_ready = [sem(f"q_ready{n}") for n in range(3)]
        q_squared = [sem(f"q_squared{n}") for n in range(3)]
        norm_summed = [sem(f"norm_summed{n}") for n in range(3)]
        norm_floored = [sem(f"norm_floored{n}") for n in range(3)]
        norm_ln_done = [sem(f"norm_ln_done{n}") for n in range(3)]
        norm_inv_done = [sem(f"norm_inv_done{n}") for n in range(3)]
        k_ready, s0_scaled, s0_done = sem("k_ready"), sem("s0_scaled"), sem("s0_done")
        kt_done, k_diag_done = sem("kt_done"), sem("k_diag_done")
        qt_done = [sem(f"qt_done{n}") for n in range(2)]
        qt_copied = [sem(f"qt_copied{n}") for n in range(2)]
        pad_neg_done, masked_bias_done = sem("pad_neg_done"), sem("masked_bias_done")
        scores_done = [sem(f"scores_done{n}") for n in range(NCH)]
        s0_placed = sem("s0_placed")
        biased = [sem(f"biased{n}") for n in range(NCH)]
        max_done = [sem(f"max_done{n}") for n in range(NCH)]
        exp_done = [sem(f"exp_done{n}") for n in range(NCH)]
        den_inv_done = [sem(f"den_inv_done{n}") for n in range(NCH)]
        probs_done = [sem(f"probs_done{n}") for n in range(NCH)]
        pt_done = [sem(f"pt_done{n}") for n in range(NCH)]
        pt_copied = [sem(f"pt_copied{n}") for n in range(NCH)]
        values_done = [sem(f"values_done{n}") for n in range(2)]
        o_hi_done = [sem(f"o_hi_done{n}") for n in range(2)]
        o_lo_done = [sem(f"o_lo_done{n}") for n in range(2)]
        y_done, bn_out_done, mv_out_done, ln_out_done, rstd_out_done, y_read = (
            sem(n) for n in ("y_done", "bn_out_done", "mv_out_done", "ln_out_done", "rstd_out_done", "y_read"))
        layer_done = [sem(f"layer_done{n}") for n in range(2)]

        sp_passed, dve_passed, pool_passed = sem("sp_passed"), sem("dve_passed"), sem("pool_passed")

        block = ctx.enter_context(nc.Block())

        @block.sync
        def _(sp):
            def load_xa(batch):
                sp.dma_start(xa[:, :], x[batch]).then_inc(xa_loaded, 16)

            def load_keep(layer, batch):
                src = (keep0, keep1)[layer][batch]
                sp.dma_start(keep[layer][:, :], src.unsqueeze(0).to_broadcast([P, S])).then_inc(keep_loaded[layer], 16)

            load_xa(0)
            load_keep(0, 0)
            load_keep(1, 0)

            def body(a, a_prev, b_old, b_new, more):
                if a and more:
                    wait_apart(sp, xn_done, a.done, sp_passed)
                    load_xa(a.batch + 1)
                if a_prev:
                    wait_apart(sp, layer_done[0], a_prev.sdone, sp_passed)
                if a:
                    sp.dma_start(x_res[:, :], x[a.batch]).then_inc(x_res_loaded, 16)
                if a and more:
                    wait_apart(sp, pad_neg_done, a.done, sp_passed)
                    load_keep(0, a.batch + 1)
                if b_old:
                    wait_apart(sp, layer_done[1], b_old.sdone, sp_passed)
                    sp.dma_start(out[b_old.batch], x_out[:, :]).then_inc(out_stored, 16)
                if b_new:
                    sp.dma_start(x1_res[:, :], x1[:, :]).then_inc(x1_copied, 16)
                    if not (isinstance(b_new.batch, int) and b_new.batch == NB - 1):
                        wait_apart(sp, pad_neg_done, b_new.done, sp_passed)
                        load_keep(1, b_new.batch + 1)

            run_units(sp, body, NB)
            sp.wait_ge(out_stored, 16 * NB)

        @block.tensor
        def _(pe):
            def transpose_x(u):
                wait(pe, xn_done, u.done)
                wait(pe, k_diag_done, u.prev)
                for c in range(KC):
                    t = nc.tensor.transpose(Q[2][:, c * P:(c + 1) * P], xn[:, c * P:(c + 1) * P], ident[:, :])
                t.then_inc(xt_done, 1)

            def project(u):
                wait(pe, x_lo_done, u.done)
                for b in (2, 0, 1):
                    if b < 2:
                        wait(pe, qt_copied[b], u.prev)
                    lo, hi = QB[b]
                    n = 0
                    for xs, ws in ((x_hi, w_hi), (x_lo, w_hi), (x_hi, w_lo)):
                        for c in range(KC):
                            m = nc.tensor.matmul(Q[b][:, 0:hi - lo], xs[:, c * P:(c + 1) * P], ws[u.layer][:, c, lo:hi],
                                                 start=(n == 0), stop=(n == 3 * KC - 1))
                            n += 1
                    m.then_inc(proj_done[b], 1)

            def transpose_q(u):
                wait(pe, k_ready, u.done)
                wait(pe, q_ready[2], u.done)
                nc.tensor.transpose(Q[2][:, 0:P], k_dup[:, :, :].rearrange("p a d -> p (a d)"), ident[:, :]).then_inc(kt_done, 1)
                wait(pe, q_ready[0], u.done)
                wait(pe, q_ready[1], u.done)
                for j in range(PAIRS):
                    t = nc.tensor.transpose(Q[j // 4][:, (j % 4) * P:(j % 4 + 1) * P], q_sb[:, j * P:(j + 1) * P], ident[:, :])
                    if j % 4 == 3:
                        t.then_inc(qt_done[j // 4], 1)

            def scores(u):
                wait(pe, k_diag_done, u.done)
                wait(pe, qt_copied[0], u.done)
                wait(pe, qt_copied[1], u.done)
                for c in range(NCH):
                    if c < 2:
                        wait(pe, pt_copied[c + 2], u.prev)
                    else:
                        wait(pe, biased[c - 2], u.done)
                    for jj in range(2):
                        j = 2 * c + jj
                        m = nc.tensor.matmul(SP[c % 2][:, jj * 2 * S:(jj + 1) * 2 * S], q_t[:, j * P:(j + 1) * P], k_diag[:, :],
                                             start=True, stop=True)
                    m.then_inc(scores_done[c], 1)

            def transpose_p(u):
                for c in range(NCH):
                    wait(pe, probs_done[c], u.done)
                    wait(pe, biased[c + 2] if c < 2 else pt_copied[c - 2], u.done)
                    for h in range(CH):
                        t = nc.tensor.transpose(SP[c % 2][:, h * S:(h + 1) * S], probs[:, c * CH + h, 0:S], ident[:, :])
                    t.then_inc(pt_done[c], 1)

            def values(u):
                for g in range(2):
                    wait(pe, pt_copied[2 * g], u.done)
                    wait(pe, pt_copied[2 * g + 1], u.done)
                    wait(pe, o_lo_done[g], u.prev)
                    for par in range(2):
                        m = nc.tensor.matmul(O[g][par * DH:(par + 1) * DH, :], v_diff[u.layer][:, :],
                                             probs[:, 8 * g + par:8 * g + 8:2, 0:S], start=True, stop=True)
                    m.then_inc(values_done[g], 1)

            def project_out(u):
                wait(pe, y_read, u.prev)
                n = 0
                for g in range(2):
                    wait(pe, o_lo_done[g], u.done)
                    for os, ws in ((o_hi, wo_hi), (o_lo, wo_hi), (o_hi, wo_lo)):
                        for j in range(4 * g, 4 * g + 4):
                            m = nc.tensor.matmul(Y[:, 0:D], os[:, j * P:(j + 1) * P], ws[u.layer][:, j, :],
                                                 start=(n == 0), stop=(n == 3 * PAIRS - 1))
                            n += 1
                m.then_inc(y_done, 1)

            def body(a, a_prev, b_old, b_new, more):
                for stage, u in ((transpose_x, a), (scores, b_old), (project, a), (transpose_p, b_old), (transpose_q, a),
                                 (values, b_old), (scores, a), (project_out, b_old), (transpose_x, b_new), (transpose_p, a),
                                 (project, b_new), (values, a), (transpose_q, b_new), (project_out, a)):
                    if u:
                        stage(u)

            run_units(pe, body, NB)

        @block.scalar
        def _(act):
            def root(var, tmp, res, ready, between, finished, u):
                wait(act, ready, u.done)
                nc.scalar.activation(tmp, var, ACT.Ln, bias=eps_col[:, 0:1]).then_inc(between, 1)
                wait(act, between, u.done)
                nc.scalar.activation(res, tmp, ACT.Exp, scale=-0.5).then_inc(finished, 1)

            def rstd_of_input(u):
                root(mv_in[:, 1:2], ln_in[:, :], rstd_in[:, :], mv_in_done, ln_in_done, rstd_in_done, u)

            def rstd_of_output(u):
                root(mv_out[:, 1:2], ln_out[:, :], rstd_out[:, :], mv_out_done, ln_out_done, rstd_out_done, u)

            def split_x(u):
                wait(act, xt_done, u.done)
                nc.scalar.copy(x_hi[:, :], Q[2][:, :]).then_inc(x_hi_done, 1)

            def take_q(u):
                if u.layer == 0:
                    for b in (0, 1):
                        lo, hi = QH[b]
                        wait(act, proj_done[b], u.done)
                        nc.scalar.copy(q_sb[:, lo * DH:hi * DH], Q[b][:, 0:(hi - lo) * DH]).then_inc(q_ready[b], 1)
                    return

                def square(b):
                    lo, hi = QH[b]
                    wait(act, proj_done[b], u.done)
                    if b == 2:
                        nc.scalar.activation(k_dup[:, 0, :], Q[2][:, KO:KO + DH], ACT.Square,
                                             accum_out=norm_sq[:, H:H + 1])
                    nc.scalar.activation(q_sb[:, lo * DH:hi * DH], Q[b][:, 0:(hi - lo) * DH],
                                         ACT.Square).then_inc(q_squared[b], 1)

                def inverse_root(b):
                    lo, hi = QH[b]
                    hi += (b == 2)
                    wait(act, norm_floored[b], u.sdone)
                    nc.scalar.activation(norm_ln[:, lo:hi], norm_sq[:, lo:hi], ACT.Ln,
                                         scale=NORM_SCALE).then_inc(norm_ln_done[b], 1)
                    wait(act, norm_ln_done[b], u.sdone)
                    nc.scalar.activation(norm_inv[:, lo:hi], norm_ln[:, lo:hi], ACT.Exp, scale=-0.5,
                                         bias=root_col[:, 0:1]).then_inc(norm_inv_done[b], 1)

                square(2)
                square(0)
                inverse_root(2)
                square(1)
                inverse_root(0)
                inverse_root(1)

            def take_qt(u):
                for g in range(2):
                    wait(act, qt_done[g], u.done)
                    nc.scalar.copy(q_t[:, g * 512:(g + 1) * 512], Q[g][:, :]).then_inc(qt_copied[g], 1)

            def exponential(u):
                for c in range(NCH):
                    wait(act, max_done[c], u.done)
                    for h in range(c * CH, (c + 1) * CH):
                        e = nc.scalar.activation(probs[:, h, :], probs[:, h, :], ACT.Exp, bias=neg_max[:, h:h + 1],
                                                 accum_out=den[:, h:h + 1])
                    e.then_inc(exp_done[c], 1)

            def take_pt(u):
                for c in range(NCH):
                    wait(act, pt_done[c], u.done)
                    nc.scalar.copy(probs[:, c * CH:(c + 1) * CH, 0:S],
                                   SP[c % 2].rearrange("p (h s) -> p h s", h=CH)).then_inc(pt_copied[c], 1)

            def split_o(u):
                for g in range(2):
                    wait(act, values_done[g], u.done)
                    nc.scalar.activation(o_hi[:, g * 512:(g + 1) * 512], O[g], ACT.Identity,
                                         bias=null_v_col[:, 0:1]).then_inc(o_hi_done[g], 1)

            def body(a, a_prev, b_old, b_new, more):
                for stage, u in ((rstd_of_input, a), (split_x, a), (exponential, b_old), (rstd_of_output, a_prev), (take_q, a),
                                 (take_pt, b_old), (take_qt, a), (split_o, b_old), (rstd_of_input, b_new), (exponential, a),
                                 (split_x, b_new), (rstd_of_output, b_old), (take_pt, a), (take_q, b_new), (split_o, a),
                                 (take_qt, b_new)):
                    if u:
                        stage(u)

            run_units(act, body, NB)

        @block.vector
        def _(dve):
            def normalise(u):
                if u.layer == 0:
                    wait(dve, xa_loaded, u.sdone * 16)
                    src = xa
                else:
                    wait(dve, layer_done[0], u.sdone)
                    src = x1
                nc.vector.bn_stats(bn_in[:, :], src[:, :]).then_inc(bn_in_done, 1)
                wait_apart(dve, bn_in_done, u.done, dve_passed)
                nc.vector.bn_aggr(mv_in[:, :], bn_in[:, :]).then_inc(mv_in_done, 1)
                wait(dve, rstd_in_done, u.done)
                wait(dve, xt_done, u.prev)
                nc.vector.tensor_scalar(xn[:, :], src[:, :], mv_in[:, 0:1], rstd_in[:, 0:1], ALU.subtract,
                                        ALU.mult).then_inc(xn_done, 1)

            def split_x(u):
                wait(dve, x_hi_done, u.done)
                nc.vector.tensor_tensor(x_lo[:, :], Q[2][:, :], x_hi[:, :].bitcast(F32), ALU.subtract).then_inc(x_lo_done, 1)

            def take_kv(u):
                kv = Q[2]
                if u.layer == 0:
                    wait(dve, proj_done[2], u.done)
                else:
                    wait(dve, q_squared[2], u.sdone)
                nc.vector.tensor_tensor(v_diff[u.layer][:, :], kv[:, VO:VO + DH], null_v[:, :], ALU.subtract)
                if u.layer == 0:
                    nc.vector.tensor_tensor(s0[0][:, :], kv[:, SO:SO + H], null_bias[0][:, :], ALU.add)
                    nc.vector.tensor_copy(k_dup[:, :, :], kv[:, KO:KO + DH].unsqueeze(1).to_broadcast([P, 2, DH])).then_inc(k_ready, 1)
                    nc.vector.tensor_copy(q_sb[:, Q2:INNER], kv[:, 0:INNER - Q2]).then_inc(q_ready[2], 1)
                    return
                nc.vector.tensor_copy(s0[1][:, :], kv[:, SO:SO + H])

                def norms(b):
                    lo, hi = QH[b]
                    wait(dve, q_squared[b], u.sdone)
                    nc.vector.tensor_reduce(norm_sq[:, lo:hi], q_sb[:, lo * DH:hi * DH].rearrange("p (h d) -> p h d", d=DH),
                                            AX.X, ALU.add).then_inc(norm_summed[b], 1)
                    wait(dve, norm_summed[b], u.sdone)
                    hi += (b == 2)
                    nc.vector.tensor_scalar(norm_sq[:, lo:hi], norm_sq[:, lo:hi], NORM_FLOOR, None,
                                            ALU.max).then_inc(norm_floored[b], 1)

                def scale(b):
                    lo, hi = QH[b]
                    wait(dve, norm_inv_done[b], u.sdone)
                    nc.vector.tensor_tensor(q_sb[:, lo * DH:hi * DH].rearrange("p (h d) -> p h d", d=DH),
                                            Q[b][:, 0:(hi - lo) * DH].rearrange("p (h d) -> p h d", d=DH),
                                            norm_inv[:, lo:hi].unsqueeze(2).to_broadcast([P, hi - lo, DH]),
                                            ALU.mult).then_inc(q_ready[b], 1)

                norms(2)
                norms(0)
                wait(dve, norm_inv_done[2], u.sdone)
                nc.vector.tensor_scalar(k_dup[:, :, :], kv[:, KO:KO + DH].unsqueeze(1).to_broadcast([P, 2, DH]),
                                        norm_inv[:, H:H + 1], None, ALU.mult).then_inc(k_ready, 1)
                scale(2)
                norms(1)
                scale(0)
                scale(1)
                nc.vector.tensor_tensor(s0[1][:, :], s0[1][:, :], norm_inv[:, 0:H], ALU.mult).then_inc(s0_scaled, 1)
                wait(dve, s0_scaled, u.sdone)
                nc.vector.tensor_tensor(s0[1][:, :], s0[1][:, :], null_bias[1][:, :], ALU.add).then_inc(s0_done, 1)

            def take_kt(u):
                wait(dve, kt_done, u.done)
                nc.vector.tensor_scalar(k_diag[0:DH, 0:S], Q[2][0:DH, 0:S], k_scale[u.layer][0:DH, 0:1], None, ALU.mult)
                nc.vector.tensor_scalar(k_diag[DH:P, S:2 * S], Q[2][DH:P, 0:S], k_scale[u.layer][DH:P, 0:1], None,
                                        ALU.mult).then_inc(k_diag_done, 1)

            def softmax(u):
                def add_bias(c):
                    wait(dve, scores_done[c], u.done)
                    nc.vector.tensor_tensor(probs[:, c * CH:(c + 1) * CH, 0:S], SP[c % 2].rearrange("p (h s) -> p h s", h=CH),
                                            masked_bias[:, c * CH:(c + 1) * CH, :], ALU.add).then_inc(biased[c], 1)

                def row_max(c):
                    wait(dve, biased[c], u.done)
                    nc.vector.tensor_reduce(neg_max[:, c * CH:(c + 1) * CH], probs[:, c * CH:(c + 1) * CH, :], AX.X, ALU.max,
                                            negate=True).then_inc(max_done[c], 1)

                def inverse(c):
                    wait(dve, exp_done[c], u.done)
                    nc.vector.reciprocal(den_inv[:, c * CH:(c + 1) * CH], den[:, c * CH:(c + 1) * CH]).then_inc(den_inv_done[c], 1)

                wait(dve, scores_done[0], u.done)
                if u.layer == 1:
                    wait(dve, s0_done, u.sdone)
                nc.vector.tensor_copy(probs[:, :, S:S + 1], s0[u.layer][:, :].unsqueeze(2)).then_inc(s0_placed, 1)
                wait(dve, masked_bias_done, u.done)
                add_bias(0)
                wait(dve, s0_placed, u.done)
                row_max(0)
                add_bias(1)
                row_max(1)
                add_bias(2)
                row_max(2)
                inverse(0)
                add_bias(3)
                row_max(3)
                for c in range(1, NCH):
                    inverse(c)

            def split_o(u):
                for g in range(2):
                    wait(dve, o_hi_done[g], u.done)
                    nc.vector.scalar_tensor_tensor(o_lo[:, g * 512:(g + 1) * 512], O[g], null_v_col[:, 0:1],
                                                   o_hi[:, g * 512:(g + 1) * 512].bitcast(F32), ALU.add,
                                                   ALU.subtract).then_inc(o_lo_done[g], 1)

            def finish(u):
                dst, res = (x1, x_res) if u.layer == 0 else (x_out, x1_res)
                wait(dve, y_done, u.done)
                nc.vector.bn_stats(bn_out[:, :], Y[:, 0:D]).then_inc(bn_out_done, 1)
                wait_apart(dve, bn_out_done, u.done, dve_passed)
                nc.vector.bn_aggr(mv_out[:, :], bn_out[:, :]).then_inc(mv_out_done, 1)
                wait(dve, mv_out_done, u.done)
                if u.layer == 0:
                    wait(dve, x1_copied, u.same * 16)
                else:
                    wait(dve, out_stored, u.same * 16)
                nc.vector.scalar_tensor_tensor(dst[:, :], Y[:, 0:D], mv_out[:, 0:1], g_out[u.layer][:, :], ALU.subtract,
                                               ALU.mult).then_inc(y_read, 1)
                wait(dve, rstd_out_done, u.done)
                wait(dve, y_read, u.done)
                wait(dve, x_res_loaded if u.layer == 0 else x1_copied, u.sdone * 16)
                nc.vector.scalar_tensor_tensor(dst[:, :], dst[:, :], rstd_out[:, 0:1], res[:, :], ALU.mult,
                                               ALU.add).then_inc(layer_done[u.layer], 1)

            def body(a, a_prev, b_old, b_new, more):
                for stage, u in ((normalise, a), (split_x, a), (softmax, b_old), (finish, a_prev), (take_kv, a), (take_kt, a),
                                 (split_o, b_old), (normalise, b_new), (softmax, a), (split_x, b_new), (finish, b_old),
                                 (take_kv, b_new), (split_o, a), (take_kt, b_new)):
                    if u:
                        stage(u)

            run_units(dve, body, NB)

        @block.gpsimd
        def _(pool):
            def mask_bias(u):
                wait(pool, keep_loaded[u.layer], u.sdone * 16)
                wait_apart(pool, masked_bias_done, u.prev, pool_passed)
                nc.gpsimd.tensor_scalar(pad_neg[:, :], keep[u.layer][:, :], -NEG, NEG, ALU.mult, ALU.add).then_inc(pad_neg_done, 1)
                wait(pool, biased[NCH - 1], u.prev)
                wait(pool, pad_neg_done, u.done)
                nc.gpsimd.tensor_tensor(masked_bias[:, :, :], bias[u.layer][:, :, :],
                                        pad_neg[:, :].unsqueeze(1).to_broadcast([P, H, S]), ALU.add).then_inc(masked_bias_done, 1)

            def divide(u):
                for c in range(NCH):
                    wait(pool, den_inv_done[c], u.done)
                    nc.gpsimd.tensor_tensor(probs[:, c * CH:(c + 1) * CH, 0:S], probs[:, c * CH:(c + 1) * CH, 0:S],
                                            den_inv[:, c * CH:(c + 1) * CH].unsqueeze(2).to_broadcast([P, CH, S]),
                                            ALU.mult).then_inc(probs_done[c], 1)

            def body(a, a_prev, b_old, b_new, more):
                for stage, u in ((divide, b_old), (mask_bias, a), (divide, a), (mask_bias, b_new)):
                    if u:
                        stage(u)

            run_units(pool, body, NB)


def setup(nc, ctx, null_kv, bias0, L0, L1, v):
    KC, COLS, INNER, DH, H, D, S, PAIRS = (v[n] for n in ("KC", "COLS", "INNER", "DH", "H", "D", "S", "PAIRS"))
    w_hi, w_lo, wo_hi, wo_lo, bias, g_out, null_bias, k_scale = (
        v[n] for n in ("w_hi", "w_lo", "wo_hi", "wo_lo", "bias", "g_out", "null_bias", "k_scale"))
    null_v, null_v_col, ident, eps_col, root_col, k_diag, psum = (
        v[n] for n in ("null_v", "null_v_col", "ident", "eps_col", "root_col", "k_diag", "psum"))
    layers = (L0, L1)
    diagonals = nc.dram_tensor("diagonals", [H, 2 * S], F32, kind="Internal").ap()

    def row(ap, n):
        return ap.unsqueeze(0).to_broadcast([P, n])

    with ExitStack() as scratch:
        def sb(name, shape, dt=F32):
            return scratch.enter_context(nc.sbuf_tensor(name, shape, dt))

        def sem(name):
            return ctx.enter_context(nc.semaphore(name))

        raw = sb("raw", [P, 2, COLS])
        prod = sb("prod", [P, INNER])
        g_in = [sb(f"g_in{n}", [P, KC]) for n in range(2)]
        null_k = sb("null_k", [P, DH])
        null_k_unit = sb("null_k_unit", [P, DH])
        null_key = [sb(f"null_key{n}", [P, DH]) for n in range(2)]
        scale_row = sb("scale_row", [P, 2, DH])
        scale_col = sb("scale_col", [P, 2])
        nk_sq = sb("nk_sq", [P, DH])
        nk = sb("nk", [P, 4])
        rows = sb("rows", [P, 6, D])
        h = sb("h", [P, D])
        sig = sb("sig", [P, D])
        h_t = sb("h_t", [P, D])
        w1 = sb("w1", [P, KC, D])
        w2 = sb("w2", [P, KC, H])
        b2 = sb("b2", [P, H])
        bn = sb("bn", [P, 6])
        mv = sb("mv", [P, 2])
        rs = sb("rs", [P, 2])
        pos = sb("pos", [P, 1])
        neg_tile = sb("neg_tile", [H, S])
        flip = sb("flip", [P, P])
        diag_sb = sb("diag_sb", [P, H])
        diag_t = sb("diag_t", [H, S])

        small_loaded, mlp_loaded = sem("small_loaded"), sem("mlp_loaded")
        raw_loaded = [sem(f"raw_loaded{n}") for n in range(2)]
        raw_read, hi_done = sem("raw_read"), sem("hi_done")
        ident_zero, ident_done, flip_done = sem("ident_zero"), sem("ident_done"), sem("flip_done")
        pool_done, causal_done = sem("pool_done"), sem("causal_done")
        dve_step, act_step, pe_step = sem("dve_step"), sem("act_step"), sem("pe_step")
        diag_stored, diag_loaded = sem("diag_stored"), sem("diag_loaded")

        small = []
        for n, L in enumerate(layers):
            small += [(g_in[n][:, :], L["g_in"].rearrange("(c p) -> p c", p=P)), (g_out[n][:, :], row(L["g_out"], D)),
                      (null_bias[n][:, :], row(L["null_bias"], H))]
        small += [(null_k[:, :], row(null_kv[0], DH)), (null_v[:, :], row(null_kv[1], DH))]
        for e in range(2):
            half = slice(e * DH, (e + 1) * DH)
            small += [(null_v_col[half, :], null_kv[1].unsqueeze(1)), (scale_col[half, 0:1], L1["q_scale"].unsqueeze(1)),
                      (scale_col[half, 1:2], L1["k_scale"].unsqueeze(1))]
        small += [(scale_row[:, 0, :], row(L1["q_scale"], DH)), (scale_row[:, 1, :], row(L1["k_scale"], DH)),
                  (bias[0][:, :, :], bias0.rearrange("h q k -> q h k"))]
        mlp = [(rows[:, n, :], row(L1[k], D)) for n, k in enumerate(("w0", "b0", "g0", "b1", "g1"))]
        mlp += [(w1[:, :, :], L1["w1"].rearrange("(c p) n -> p c n", p=P)), (w2[:, :, :], L1["w2"].rearrange("(c p) n -> p c n", p=P)),
                (b2[:, :], row(L1["b2"], H))]
        pieces = [("in", n, c) for n in range(2) for c in range(KC)] + [("out", n, c) for n in range(2) for c in range(PAIRS // 2)]

        with nc.Block() as block:
            marks = {}
            split_ready, diag_computed, flipped = sem("split_ready"), sem("diag_computed"), sem("flipped")

            def piece_aps(i, kind, n, c):
                if kind == "in":
                    return raw[:, i % 2, :], w_hi[n][:, c, :], w_lo[n][:, c, :]
                flat = lambda t: t[n][:, 2 * c:2 * c + 2, :].rearrange("p a d -> p (a d)")
                return raw[:, i % 2, 0:2 * D], flat(wo_hi), flat(wo_lo)

            @block.vector
            def _(dve):
                V = nc.vector
                count = [0]

                def step(ins, mark=None):
                    ins.then_inc(dve_step, 1)
                    count[0] += 1
                    dve.wait_ge(dve_step, count[0])
                    marks[mark] = count[0]

                step(V.memset(k_diag[:, :], 0.0))
                step(V.memset(eps_col[:, :], EPS))
                step(V.memset(root_col[:, :], LN_NORM_ROOT))
                step(V.memset(k_scale[0][:, :], DH ** -0.5))
                dve.wait_ge(small_loaded, 16 * len(small))
                step(V.scalar_tensor_tensor(k_scale[1][:, :], scale_col[:, 0:1], 8.0, scale_col[:, 1:2], ALU.mult, ALU.mult))
                step(V.tensor_scalar(null_key[0][:, :], null_k[:, :], DH ** -0.5, None, ALU.mult))
                step(V.tensor_tensor(nk_sq[:, :], null_k[:, :], null_k[:, :], ALU.mult))
                step(V.tensor_reduce(nk[:, 0:1], nk_sq[:, :], AX.X, ALU.add))
                step(V.tensor_scalar(nk[:, 1:2], nk[:, 0:1], NORM_FLOOR, None, ALU.max), "null key's norm")
                dve.wait_ge(act_step, 2)
                step(V.tensor_scalar(null_k_unit[:, :], null_k[:, :], nk[:, 3:4], None, ALU.mult))
                step(V.scalar_tensor_tensor(nk_sq[:, :], scale_row[:, 0, :], 8.0, scale_row[:, 1, :], ALU.mult, ALU.mult))
                step(V.tensor_tensor(null_key[1][:, :], null_k_unit[:, :], nk_sq[:, :], ALU.mult))

                dve.wait_ge(mlp_loaded, 16 * len(mlp))
                dve.wait_ge(pool_done, 2)
                step(V.tensor_scalar(h[:, :], rows[:, 0, :], pos[:, 0:1], None, ALU.mult))
                step(V.tensor_tensor(h[:, :], h[:, :], rows[:, 1, :], ALU.add))

                def norm_silu(layer, gain):
                    step(V.bn_stats(bn[:, :], h[:, :]))
                    step(V.bn_aggr(mv[:, :], bn[:, :]), f"statistics {layer}")
                    step(V.scalar_tensor_tensor(h[:, :], h[:, :], mv[:, 0:1], gain, ALU.subtract, ALU.mult))
                    dve.wait_ge(act_step, 4 + 3 * layer)
                    step(V.tensor_scalar(h[:, :], h[:, :], rs[:, 1:2], None, ALU.mult), f"normed {layer}")
                    dve.wait_ge(act_step, 5 + 3 * layer)
                    step(V.tensor_scalar(sig[:, :], sig[:, :], 1.0, None, ALU.add))
                    step(V.reciprocal(sig[:, :], sig[:, :]))
                    step(V.tensor_tensor(h[:, :], h[:, :], sig[:, :], ALU.mult), f"silu {layer}")

                norm_silu(0, rows[:, 2, :])
                dve.wait_ge(pe_step, 1)
                step(V.tensor_copy(h_t[:, :], psum[:, 0, :]), "silu^T 0")
                dve.wait_ge(pe_step, 2)
                step(V.tensor_tensor(h[:, :], psum[:, 1, :], rows[:, 3, :], ALU.add))
                norm_silu(1, rows[:, 4, :])
                dve.wait_ge(pe_step, 3)
                step(V.tensor_copy(h_t[:, :], psum[:, 0, :]), "silu^T 1")
                dve.wait_ge(pe_step, 4)
                step(V.tensor_tensor(diag_sb[:, :], psum[:, 1, 0:H], b2[:, :], ALU.add), "diagonals")
                dve.wait_ge(pe_step, 5)
                V.tensor_copy(diag_t[:, :], psum[0:H, 2, 0:S]).then_inc(diag_computed, 1)

                for i, (kind, n, c) in enumerate(pieces):
                    dve.wait_ge(raw_loaded[i % 2], 32 * (i // 2 + 1))
                    src, hi, lo = piece_aps(i, kind, n, c)
                    w = raw[:, i % 2, :]
                    if kind == "in":
                        step(V.tensor_scalar(w[:, 0:INNER + 2 * DH], w[:, 0:INNER + 2 * DH], g_in[n][:, c:c + 1], None, ALU.mult))
                        step(V.tensor_tensor(prod[:, :].rearrange("p (h d) -> p h d", d=DH), w[:, 0:INNER].rearrange("p (h d) -> p h d", d=DH),
                                             null_key[n][:, :].unsqueeze(1).to_broadcast([P, H, DH]), ALU.mult))
                        step(V.tensor_reduce(w[:, INNER + 2 * DH:COLS], prod[:, :].rearrange("p (h d) -> p h d", d=DH), AX.X, ALU.add))
                    V.engine_nop().then_inc(split_ready, 1)
                    dve.wait_ge(hi_done, i + 1)
                    V.tensor_tensor(lo, src, hi.bitcast(F32), ALU.subtract).then_inc(raw_read, 1)
                dve.wait_ge(raw_read, len(pieces))

            @block.sync
            def _(sp):
                for dst, src in small:
                    sp.dma_start(dst, src, allow_slow_non_contiguous=True).then_inc(small_loaded, 16)
                for i, (kind, n, c) in enumerate(pieces):
                    if i >= 2:
                        sp.wait_ge(raw_read, i - 1)
                    L, slot = layers[n], i % 2
                    if kind == "in":
                        sp.dma_start(raw[:, slot, 0:INNER], L["Wq"][c * P:(c + 1) * P, :]).then_inc(raw_loaded[slot], 16)
                        sp.dma_start(raw[:, slot, INNER:INNER + 2 * DH], L["Wkv"][c * P:(c + 1) * P, :]).then_inc(raw_loaded[slot], 16)
                    else:
                        for k in range(2):
                            j = 2 * c + k
                            sp.dma_start(raw[:, slot, k * D:(k + 1) * D], L["Wo"][j * P:(j + 1) * P, :]).then_inc(raw_loaded[slot], 16)

            @block.scalar
            def _(act):
                for dst, src in mlp:
                    act.dma_start(dst, src).then_inc(mlp_loaded, 16)
                count = [0]

                def step(need, ins_of):
                    act.wait_ge(dve_step, marks[need])
                    ins_of().then_inc(act_step, 1)
                    count[0] += 1
                    act.wait_ge(act_step, count[0])

                step("null key's norm", lambda: nc.scalar.activation(nk[:, 2:3], nk[:, 1:2], ACT.Ln, scale=NORM_SCALE))
                step("null key's norm", lambda: nc.scalar.activation(nk[:, 3:4], nk[:, 2:3], ACT.Exp, scale=-0.5, bias=root_col[:, 0:1]))
                for layer in range(2):
                    step(f"statistics {layer}", lambda: nc.scalar.activation(rs[:, 0:1], mv[:, 1:2], ACT.Ln, bias=eps_col[:, 0:1]))
                    step(f"statistics {layer}", lambda: nc.scalar.activation(rs[:, 1:2], rs[:, 0:1], ACT.Exp, scale=-0.5))
                    step(f"normed {layer}", lambda: nc.scalar.activation(sig[:, :], h[:, :], ACT.Exp, scale=-1.0))
                for i, (kind, n, c) in enumerate(pieces):
                    act.wait_ge(split_ready, i + 1)
                    src, hi, _ = piece_aps(i, kind, n, c)
                    nc.scalar.copy(hi, src).then_inc(hi_done, 1)
                act.wait_ge(diag_computed, 1)
                act.dma_start(diagonals[:, 0:S], diag_t[:, :]).then_inc(diag_stored, 16)
                act.dma_start(diagonals[:, S:2 * S], neg_tile[:, :]).then_inc(diag_stored, 16)
                act.wait_ge(diag_stored, 32)
                act.dma_start(bias[1][:, :, :], bass.AP(diagonals.tensor, 0, [[1, P], [2 * S, H], [1, S]])).then_inc(diag_loaded, 16)
                for c in range(4):
                    act.wait_ge(flipped, c + 1)
                    nc.scalar.copy(bias[1][:, 4 * c:4 * c + 4, :], psum[:, 3 + c, :].rearrange("p (h s) -> p h s", h=4))

            @block.gpsimd
            def _(pool):
                nc.gpsimd.memset(ident[:, :], 0.0).then_inc(ident_zero, 1)
                pool.wait_ge(ident_zero, 1)
                nc.gpsimd.affine_select(out=ident[:, :], in_=ident[:, :], compare_op=ALU.not_equal, fill=1.0, base=0,
                                        pattern=[[-1, P]], channel_multiplier=1).then_inc(ident_done, 1)
                nc.gpsimd.memset(flip[:, :], 0.0).then_inc(ident_zero, 1)
                pool.wait_ge(ident_zero, 2)
                nc.gpsimd.affine_select(out=flip[:, :], in_=flip[:, :], compare_op=ALU.not_equal, fill=1.0, base=1 - S,
                                        pattern=[[1, P]], channel_multiplier=1).then_inc(flip_done, 1)
                nc.gpsimd.iota(pos[:, :], pattern=[[0, 1]], base=S - 1, channel_multiplier=-1,
                               allow_small_or_imprecise_dtypes=True).then_inc(pool_done, 1)
                nc.gpsimd.memset(neg_tile[:, :], NEG).then_inc(pool_done, 1)
                pool.wait_ge(small_loaded, 16 * len(small))
                nc.gpsimd.affine_select(out=bias[0][:, :, :], in_=bias[0][:, :, :], compare_op=ALU.is_ge, fill=NEG, base=0,
                                        pattern=[[0, H], [-1, S]], channel_multiplier=1).then_inc(causal_done, 1)
                pool.wait_ge(causal_done, 1)

            @block.tensor
            def _(pe):
                pe.wait_ge(ident_done, 1)

                def transposed_h(layer):
                    pe.wait_ge(dve_step, marks[f"silu {layer}"])
                    for c in range(KC):
                        t = nc.tensor.transpose(psum[:, 0, c * P:(c + 1) * P], h[:, c * P:(c + 1) * P], ident[:, :])
                    t.then_inc(pe_step, 1)

                transposed_h(0)
                pe.wait_ge(dve_step, marks["silu^T 0"])
                for c in range(KC):
                    m = nc.tensor.matmul(psum[:, 1, :], h_t[:, c * P:(c + 1) * P], w1[:, c, :], start=(c == 0), stop=(c == KC - 1))
                m.then_inc(pe_step, 1)
                transposed_h(1)
                pe.wait_ge(dve_step, marks["silu^T 1"])
                for c in range(KC):
                    m = nc.tensor.matmul(psum[:, 1, 0:H], h_t[:, c * P:(c + 1) * P], w2[:, c, :], start=(c == 0), stop=(c == KC - 1))
                m.then_inc(pe_step, 1)
                pe.wait_ge(dve_step, marks["diagonals"])
                nc.tensor.transpose(psum[0:H, 2, 0:S], diag_sb[:, :], ident[:, :]).then_inc(pe_step, 1)
                pe.wait_ge(flip_done, 1)
                pe.wait_ge(diag_loaded, 16)
                for c in range(4):
                    nc.tensor.matmul(psum[:, 3 + c, :], flip[:, :], bias[1][:, 4 * c:4 * c + 4, :].rearrange("p h s -> p (h s)"),
                                     start=True, stop=True).then_inc(flipped, 1)


_COMMON = ["x", "fside_16xSxS_0", "cond_64", "mask_BxS_bk0", "mask_BxS_bf1"]
_L0 = {"g_in": "g_in", "null_bias": "null_attn_bias", "Wq": "Wq", "Wkv": "Wkv", "Wo": "Wo", "g_out": "g_out"}
_L1 = {"g_in": "g_norm", "null_bias": "null_attn_bias", "Wq": "Wq", "Wkv": "Wkv", "Wo": "Wout", "g_out": "g_out",
       "q_scale": "q_scale", "k_scale": "k_scale", "w0": "w0", "b0": "b0", "g0": "g0", "w1": "w1", "b1": "b1", "g1": "g1",
       "w2": "w2", "b2": "b2"}


def kernel(**inputs):
    import numpy as _np
    import concourse.bacc as _bacc
    from concourse import mybir as _mybir
    from concourse.bass_utils import run_bass_kernel_spmd as _run

    nc = _bacc.Bacc("TRN2", target_bir_lowering=False, num_devices=1,
                    dynamic_dma_scratch_size=1024)
    arrays = {}

    def give(name):
        a = _np.ascontiguousarray(inputs[name])
        if name == "L1_cond_w0":
            a = a.reshape(-1)
        arrays[f"in_{name}_dram"] = a
        return nc.dram_tensor(f"in_{name}_dram", a.shape, _mybir.dt.from_np(a.dtype), kind="ExternalInput").ap()

    x, bias0, null_kv, keep0, keep1 = (give(n) for n in _COMMON)
    L0 = {k: give("L0_cond_" + n) for k, n in _L0.items()}
    L1 = {k: give("L1_cond_" + n) for k, n in _L1.items()}
    out = nc.dram_tensor("out_0_dram", inputs["x"].shape, F32, kind="ExternalOutput").ap()
    build(nc, x, bias0, null_kv, keep0, keep1, L0, L1, out)
    r = _run(nc, [arrays], core_ids=[0])
    return r.results[0]["out_0_dram"]
```

```python
from contextlib import ExitStack

import concourse.bass as bass
from concourse import mybir

F32 = mybir.dt.float32
F32R = mybir.dt.float32r
U8 = mybir.dt.uint8
ALU = mybir.AluOpType
ACT = mybir.ActivationFunctionType
AX = mybir.AxisListType

P = 128
EPS = 1e-5
NEG = -1e38
NORM_FLOOR = 1e-24
NORM_SCALE = 2.0 ** 16
LN_NORM_ROOT = 8 * 0.6931471805599453


class Unit:

    def __init__(self, layer, batch, done, prev, same, sdone):
        self.layer, self.batch, self.done, self.prev, self.same, self.sdone = layer, batch, done, prev, same, sdone


def static_unit(layer, batch, nb):
    if layer == 0:
        u = 0 if batch == 0 else 2 * batch - 1
    else:
        u = 2 * batch + 2 if batch < nb - 1 else 2 * nb - 1
    return Unit(layer, batch, u + 1, u, batch, batch + 1)


def wait(eng, sem, value):
    if isinstance(value, int) and value <= 0:
        return
    eng.wait_ge(sem, value)


def wait_apart(eng, sem, value, passed):
    if not isinstance(value, int):
        eng.wait_ge(sem, value)
        eng.sem_inc(passed, 1)
    else:
        wait(eng, sem, value)


def run_units(eng, body, nb):
    A = lambda a: static_unit(0, a, nb)
    B = lambda b: static_unit(1, b, nb)
    body(None, None, A(0), None, None)
    body(A(0), None, A(1), None, None)
    body(A(1), A(0), A(2), None, B(0))
    body(A(2), A(1), A(3), B(0), B(1))
    with eng.Fori(3, nb - 1) as i:
        twice = {k: eng.snap(i * 2 + k) for k in range(-3, 3)}
        once = {k: eng.snap(i + k) for k in (-2, -1, 1, 2)}
        once[0] = i
        a, a_prev, a_next = (Unit(0, once[k], twice[2 * k], twice[2 * k - 1], once[k], once[k + 1]) for k in (0, -1, 1))
        b_old = Unit(1, once[-2], twice[-1], twice[-2], once[-2], once[-1])
        b_new = Unit(1, once[-1], twice[1], twice[0], once[-1], once[0])
        body(a, a_prev, a_next, b_old, b_new)
    body(A(nb - 1), A(nb - 2), None, B(nb - 3), B(nb - 2))
    body(None, A(nb - 1), None, B(nb - 2), B(nb - 1))
    body(None, None, None, B(nb - 1), None)


def run_stages(*stages):
    for stage, u in stages:
        if u:
            stage(u)


def build(nc, x, bias0, null_kv, keep0, keep1, L0, L1, out):
    NB, S, D = x.shape
    H = bias0.shape[0]
    INNER = L0["Wq"].shape[1]
    DH = INNER // H
    KC = D // P
    PAIRS = H // 2
    COLS = INNER + 2 * DH + H
    HG = 6
    QB = [(0, HG * DH), (HG * DH, 2 * HG * DH), (2 * HG * DH, COLS)]
    QH = [(0, HG), (HG, 2 * HG), (2 * HG, H)]
    Q2 = 2 * HG * DH
    KO, VO, SO = INNER - Q2, INNER - Q2 + DH, INNER - Q2 + 2 * DH
    CH = 4
    NCH = H // CH
    assert S == P and DH == 64 and COLS - Q2 <= 512 and D == 512

    ctx = ExitStack()
    with ctx:
        def sb(name, shape, dt=F32, where=ctx):
            return where.enter_context(nc.sbuf_tensor(name, shape, dt))

        def sem(name):
            return ctx.enter_context(nc.semaphore(name))

        psum = ctx.enter_context(nc.psum_tensor("psum", [P, 8, 512], F32))
        Q = [psum[:, b, :] for b in range(3)]
        SP = [psum[:, 3 + b, :] for b in range(2)]
        O = [psum[:, 5 + b, :] for b in range(2)]
        Y = psum[:, 7, :]

        w_hi = [sb(f"w_hi{n}", [P, KC, COLS], F32R) for n in range(2)]
        w_lo = [sb(f"w_lo{n}", [P, KC, COLS], F32R) for n in range(2)]
        wo_hi = [sb(f"wo_hi{n}", [P, PAIRS, D], F32R) for n in range(2)]
        wo_lo = [sb(f"wo_lo{n}", [P, PAIRS, D], F32R) for n in range(2)]
        bias = [sb(f"bias{n}", [P, H, S]) for n in range(2)]
        g_out = [sb(f"g_out{n}", [P, D]) for n in range(2)]
        null_bias = [sb(f"null_bias{n}", [P, H]) for n in range(2)]
        k_scale = [sb(f"k_scale{n}", [P, 1]) for n in range(2)]
        null_v = sb("null_v", [P, DH])
        null_v_col = sb("null_v_col", [P, 1])
        ident = sb("ident", [P, P])
        eps_col = sb("eps_col", [P, 1])
        root_col = sb("root_col", [P, 1])
        k_diag = sb("k_diag", [P, 2 * S])

        setup(nc, ctx, null_kv, bias0, L0, L1, dict(
            KC=KC, COLS=COLS, INNER=INNER, DH=DH, H=H, D=D, S=S, PAIRS=PAIRS, w_hi=w_hi, w_lo=w_lo, wo_hi=wo_hi, wo_lo=wo_lo,
            bias=bias, g_out=g_out, null_bias=null_bias, k_scale=k_scale, null_v=null_v, null_v_col=null_v_col, ident=ident,
            eps_col=eps_col, root_col=root_col, k_diag=k_diag, psum=psum))

        xa = sb("xa", [P, D])
        x_res = sb("x_res", [P, D])
        x1 = sb("x1", [P, D])
        x1_res = sb("x1_res", [P, D])
        x_out = sb("x_out", [P, D])
        xn = sb("xn", [P, D])
        x_hi = sb("x_hi", [P, D], F32R)
        x_lo = sb("x_lo", [P, D], F32R)
        q_sb = sb("q_sb", [P, INNER])
        q_t = sb("q_t", [P, INNER])
        k_dup = sb("k_dup", [P, 2, DH])
        v_diff = [sb(f"v_diff{n}", [P, DH]) for n in range(2)]
        s0 = [sb(f"s0_{n}", [P, H]) for n in range(2)]
        masked_bias = sb("masked_bias", [P, H, S])
        pad_neg = sb("pad_neg", [P, S])
        keep = [sb(f"keep{n}", [P, S], U8) for n in range(2)]
        probs = sb("probs", [P, H, S + 1])
        o_hi = sb("o_hi", [P, PAIRS * P], F32R)
        o_lo = sb("o_lo", [P, PAIRS * P], F32R)
        bn_in = sb("bn_in", [P, 6])
        mv_in = sb("mv_in", [P, 2])
        rstd_in = sb("rstd_in", [P, 1])
        ln_in = sb("ln_in", [P, 1])
        bn_out = sb("bn_out", [P, 6])
        mv_out = sb("mv_out", [P, 2])
        rstd_out = sb("rstd_out", [P, 1])
        ln_out = sb("ln_out", [P, 1])
        norm_sq = sb("norm_sq", [P, H + 1])
        norm_ln = sb("norm_ln", [P, H + 1])
        norm_inv = sb("norm_inv", [P, H + 1])
        neg_max = sb("neg_max", [P, H])
        den = sb("den", [P, H])
        den_inv = sb("den_inv", [P, H])

        xa_loaded, x_res_loaded = sem("xa_loaded"), sem("x_res_loaded")
        keep_loaded = [sem(f"keep_loaded{n}") for n in range(2)]
        x1_copied, out_stored = sem("x1_copied"), sem("out_stored")
        bn_in_done, mv_in_done, ln_in_done, rstd_in_done = (sem(n) for n in ("bn_in_done", "mv_in_done", "ln_in_done", "rstd_in_done"))
        xn_done, xt_done, x_hi_done, x_lo_done = (sem(n) for n in ("xn_done", "xt_done", "x_hi_done", "x_lo_done"))
        proj_done = [sem(f"proj_done{n}") for n in range(3)]
        q_ready = [sem(f"q_ready{n}") for n in range(3)]
        q_squared = [sem(f"q_squared{n}") for n in range(3)]
        norm_summed = [sem(f"norm_summed{n}") for n in range(3)]
        norm_floored = [sem(f"norm_floored{n}") for n in range(3)]
        norm_ln_done = [sem(f"norm_ln_done{n}") for n in range(3)]
        norm_inv_done = [sem(f"norm_inv_done{n}") for n in range(3)]
        k_ready, s0_scaled, s0_done = sem("k_ready"), sem("s0_scaled"), sem("s0_done")
        kt_done, k_diag_done = sem("kt_done"), sem("k_diag_done")
        qt_done = [sem(f"qt_done{n}") for n in range(2)]
        qt_copied = [sem(f"qt_copied{n}") for n in range(2)]
        pad_neg_done, masked_bias_done = sem("pad_neg_done"), sem("masked_bias_done")
        scores_done = [sem(f"scores_done{n}") for n in range(NCH)]
        s0_placed = sem("s0_placed")
        biased = [sem(f"biased{n}") for n in range(NCH)]
        max_done = [sem(f"max_done{n}") for n in range(NCH)]
        exp_done = [sem(f"exp_done{n}") for n in range(NCH)]
        den_inv_done = [sem(f"den_inv_done{n}") for n in range(NCH)]
        probs_done = [sem(f"probs_done{n}") for n in range(NCH)]
        pt_done = [sem(f"pt_done{n}") for n in range(NCH)]
        pt_copied = [sem(f"pt_copied{n}") for n in range(NCH)]
        values_done = [sem(f"values_done{n}") for n in range(2)]
        o_hi_done = [sem(f"o_hi_done{n}") for n in range(2)]
        o_lo_done = [sem(f"o_lo_done{n}") for n in range(2)]
        y_done, bn_out_done, mv_out_done, ln_out_done, rstd_out_done, y_read = (
            sem(n) for n in ("y_done", "bn_out_done", "mv_out_done", "ln_out_done", "rstd_out_done", "y_read"))
        layer_done = [sem(f"layer_done{n}") for n in range(2)]

        sp_passed, dve_passed, pool_passed = sem("sp_passed"), sem("dve_passed"), sem("pool_passed")

        block = ctx.enter_context(nc.Block())

        @block.sync
        def _(sp):
            def load_xa(batch):
                sp.dma_start(xa[:, :], x[batch]).then_inc(xa_loaded, 16)

            def load_keep(layer, batch):
                src = (keep0, keep1)[layer][batch]
                sp.dma_start(keep[layer][:, :], src.unsqueeze(0).to_broadcast([P, S])).then_inc(keep_loaded[layer], 16)

            load_xa(0)
            load_keep(0, 0)
            load_keep(1, 0)

            def body(a, a_prev, a_next, b_old, b_new):
                if a and a_next:
                    wait_apart(sp, xn_done, a.done, sp_passed)
                    load_xa(a.batch + 1)
                if a_prev:
                    wait_apart(sp, layer_done[0], a_prev.sdone, sp_passed)
                if a:
                    sp.dma_start(x_res[:, :], x[a.batch]).then_inc(x_res_loaded, 16)
                if a and a_next:
                    wait_apart(sp, pad_neg_done, a.done, sp_passed)
                    load_keep(0, a.batch + 1)
                if b_old:
                    wait_apart(sp, layer_done[1], b_old.sdone, sp_passed)
                    sp.dma_start(out[b_old.batch], x_out[:, :]).then_inc(out_stored, 16)
                if b_new:
                    sp.dma_start(x1_res[:, :], x1[:, :]).then_inc(x1_copied, 16)
                    if not (isinstance(b_new.batch, int) and b_new.batch == NB - 1):
                        wait_apart(sp, pad_neg_done, b_new.done, sp_passed)
                        load_keep(1, b_new.batch + 1)

            run_units(sp, body, NB)
            sp.wait_ge(out_stored, 16 * NB)

        @block.tensor
        def _(pe):
            def transpose_x(u):
                wait(pe, xn_done, u.done)
                wait(pe, k_diag_done, u.prev)
                for c in range(KC):
                    t = nc.tensor.transpose(Q[2][:, c * P:(c + 1) * P], xn[:, c * P:(c + 1) * P], ident[:, :])
                t.then_inc(xt_done, 1)

            def project(u, banks=(2, 0, 1)):
                wait(pe, x_lo_done, u.done)
                for b in banks:
                    if b < 2:
                        wait(pe, qt_copied[b], u.prev)
                    lo, hi = QB[b]
                    n = 0
                    for xs, ws in ((x_hi, w_hi), (x_lo, w_hi), (x_hi, w_lo)):
                        for c in range(KC):
                            m = nc.tensor.matmul(Q[b][:, 0:hi - lo], xs[:, c * P:(c + 1) * P], ws[u.layer][:, c, lo:hi],
                                                 start=(n == 0), stop=(n == 3 * KC - 1))
                            n += 1
                    m.then_inc(proj_done[b], 1)

            def transpose_q(u):
                wait(pe, k_ready, u.done)
                wait(pe, q_ready[2], u.done)
                nc.tensor.transpose(Q[2][:, 0:P], k_dup[:, :, :].rearrange("p a d -> p (a d)"), ident[:, :]).then_inc(kt_done, 1)
                wait(pe, q_ready[0], u.done)
                wait(pe, q_ready[1], u.done)
                for j in range(PAIRS):
                    t = nc.tensor.transpose(Q[j // 4][:, (j % 4) * P:(j % 4 + 1) * P], q_sb[:, j * P:(j + 1) * P], ident[:, :])
                    if j % 4 == 3:
                        t.then_inc(qt_done[j // 4], 1)

            def scores(u):
                wait(pe, k_diag_done, u.done)
                wait(pe, qt_copied[0], u.done)
                wait(pe, qt_copied[1], u.done)
                for c in range(NCH):
                    if c < 2:
                        wait(pe, pt_copied[c + 2], u.prev)
                    else:
                        wait(pe, biased[c - 2], u.done)
                    for jj in range(2):
                        j = 2 * c + jj
                        m = nc.tensor.matmul(SP[c % 2][:, jj * 2 * S:(jj + 1) * 2 * S], q_t[:, j * P:(j + 1) * P], k_diag[:, :],
                                             start=True, stop=True)
                    m.then_inc(scores_done[c], 1)

            def transpose_p(u):
                for c in range(NCH):
                    wait(pe, probs_done[c], u.done)
                    wait(pe, biased[c + 2] if c < 2 else pt_copied[c - 2], u.done)
                    for h in range(CH):
                        t = nc.tensor.transpose(SP[c % 2][:, h * S:(h + 1) * S], probs[:, c * CH + h, 0:S], ident[:, :])
                    t.then_inc(pt_done[c], 1)

            def values(u):
                for g in range(2):
                    wait(pe, pt_copied[2 * g], u.done)
                    wait(pe, pt_copied[2 * g + 1], u.done)
                    wait(pe, o_lo_done[g], u.prev)
                    for par in range(2):
                        m = nc.tensor.matmul(O[g][par * DH:(par + 1) * DH, :], v_diff[u.layer][:, :],
                                             probs[:, 8 * g + par:8 * g + 8:2, 0:S], start=True, stop=True)
                    m.then_inc(values_done[g], 1)

            def project_out(u, halves=(0, 1)):
                n = 3 * PAIRS // 2 * halves[0]
                if n == 0:
                    wait(pe, y_read, u.prev)
                for g in halves:
                    wait(pe, o_lo_done[g], u.done)
                    for os, ws in ((o_hi, wo_hi), (o_lo, wo_hi), (o_hi, wo_lo)):
                        for j in range(4 * g, 4 * g + 4):
                            m = nc.tensor.matmul(Y[:, 0:D], os[:, j * P:(j + 1) * P], ws[u.layer][:, j, :],
                                                 start=(n == 0), stop=(n == 3 * PAIRS - 1))
                            n += 1
                if n == 3 * PAIRS:
                    m.then_inc(y_done, 1)

            def body(a, a_prev, a_next, b_old, b_new):
                run_stages((transpose_x, a), (scores, b_old), (lambda u: project_out(u, (1,)), a_prev), (project, a),
                           (transpose_p, b_old), (transpose_q, a), (values, b_old), (scores, a), (transpose_x, b_new),
                           (project_out, b_old), (lambda u: project(u, (2,)), b_new), (transpose_p, a),
                           (lambda u: project(u, (0, 1)), b_new), (values, a), (transpose_q, b_new),
                           (lambda u: project_out(u, (0,)), a))

            run_units(pe, body, NB)

        @block.scalar
        def _(act):
            def root(var, tmp, res, ready, between, finished, u):
                wait(act, ready, u.done)
                nc.scalar.activation(tmp, var, ACT.Ln, bias=eps_col[:, 0:1]).then_inc(between, 1)
                wait(act, between, u.done)
                nc.scalar.activation(res, tmp, ACT.Exp, scale=-0.5).then_inc(finished, 1)

            def rstd_of_input(u):
                root(mv_in[:, 1:2], ln_in[:, :], rstd_in[:, :], mv_in_done, ln_in_done, rstd_in_done, u)

            def rstd_of_output(u):
                root(mv_out[:, 1:2], ln_out[:, :], rstd_out[:, :], mv_out_done, ln_out_done, rstd_out_done, u)

            def split_x(u):
                wait(act, xt_done, u.done)
                nc.scalar.copy(x_hi[:, :], Q[2][:, :]).then_inc(x_hi_done, 1)

            def take_q(u):
                for b in (0, 1):
                    lo, hi = QH[b]
                    wait(act, proj_done[b], u.done)
                    nc.scalar.copy(q_sb[:, lo * DH:hi * DH], Q[b][:, 0:(hi - lo) * DH]).then_inc(q_ready[b], 1)

            def square(b):
                def stage(u):
                    lo, hi = QH[b]
                    wait(act, proj_done[b], u.done)
                    if b == 2:
                        nc.scalar.activation(k_dup[:, 0, :], Q[2][:, KO:KO + DH], ACT.Square,
                                             accum_out=norm_sq[:, H:H + 1])
                    nc.scalar.activation(q_sb[:, lo * DH:hi * DH], Q[b][:, 0:(hi - lo) * DH],
                                         ACT.Square).then_inc(q_squared[b], 1)
                return stage

            def inverse_root(b):
                def stage(u):
                    lo, hi = QH[b]
                    hi += (b == 2)
                    wait(act, norm_floored[b], u.sdone)
                    nc.scalar.activation(norm_ln[:, lo:hi], norm_sq[:, lo:hi], ACT.Ln,
                                         scale=NORM_SCALE).then_inc(norm_ln_done[b], 1)
                    wait(act, norm_ln_done[b], u.sdone)
                    nc.scalar.activation(norm_inv[:, lo:hi], norm_ln[:, lo:hi], ACT.Exp, scale=-0.5,
                                         bias=root_col[:, 0:1]).then_inc(norm_inv_done[b], 1)
                return stage

            def take_qt(u):
                for g in range(2):
                    wait(act, qt_done[g], u.done)
                    nc.scalar.copy(q_t[:, g * 512:(g + 1) * 512], Q[g][:, :]).then_inc(qt_copied[g], 1)

            def exponential(u, middle=None):
                for c in range(NCH):
                    if c == 2 and middle:
                        middle()
                    wait(act, max_done[c], u.done)
                    for h in range(c * CH, (c + 1) * CH):
                        e = nc.scalar.activation(probs[:, h, :], probs[:, h, :], ACT.Exp, bias=neg_max[:, h:h + 1],
                                                 accum_out=den[:, h:h + 1])
                    e.then_inc(exp_done[c], 1)

            def take_pt(u):
                for c in range(NCH):
                    wait(act, pt_done[c], u.done)
                    nc.scalar.copy(probs[:, c * CH:(c + 1) * CH, 0:S],
                                   SP[c % 2].rearrange("p (h s) -> p h s", h=CH)).then_inc(pt_copied[c], 1)

            def split_o(u):
                for g in range(2):
                    wait(act, values_done[g], u.done)
                    nc.scalar.activation(o_hi[:, g * 512:(g + 1) * 512], O[g], ACT.Identity,
                                         bias=null_v_col[:, 0:1]).then_inc(o_hi_done[g], 1)

            def body(a, a_prev, a_next, b_old, b_new):
                run_stages((split_x, a), (exponential, b_old), (rstd_of_output, a_prev), (take_q, a), (rstd_of_input, b_new),
                           (take_pt, b_old), (take_qt, a), (split_o, b_old),
                           (lambda u: exponential(u, lambda: run_stages((split_x, b_new))), a))
                if not a:
                    run_stages((split_x, b_new))
                run_stages((rstd_of_output, b_old), (square(2), b_new), (take_pt, a), (inverse_root(2), b_new),
                           (rstd_of_input, a_next), (square(0), b_new), (inverse_root(0), b_new), (square(1), b_new),
                           (inverse_root(1), b_new), (split_o, a), (take_qt, b_new))

            run_units(act, body, NB)

        @block.vector
        def _(dve):
            def input_statistics(u):
                if u.layer == 0:
                    wait(dve, xa_loaded, u.sdone * 16)
                else:
                    wait(dve, layer_done[0], u.sdone)
                nc.vector.bn_stats(bn_in[:, :], (xa, x1)[u.layer][:, :]).then_inc(bn_in_done, 1)
                wait_apart(dve, bn_in_done, u.done, dve_passed)
                nc.vector.bn_aggr(mv_in[:, :], bn_in[:, :]).then_inc(mv_in_done, 1)

            def normalise(u):
                wait(dve, rstd_in_done, u.done)
                wait(dve, xt_done, u.prev)
                nc.vector.tensor_scalar(xn[:, :], (xa, x1)[u.layer][:, :], mv_in[:, 0:1], rstd_in[:, 0:1], ALU.subtract,
                                        ALU.mult).then_inc(xn_done, 1)

            def split_x(u):
                wait(dve, x_hi_done, u.done)
                nc.vector.tensor_tensor(x_lo[:, :], Q[2][:, :], x_hi[:, :].bitcast(F32), ALU.subtract).then_inc(x_lo_done, 1)

            def take_kv(u):
                kv = Q[2]
                if u.layer == 0:
                    wait(dve, proj_done[2], u.done)
                else:
                    wait(dve, q_squared[2], u.sdone)
                nc.vector.tensor_tensor(v_diff[u.layer][:, :], kv[:, VO:VO + DH], null_v[:, :], ALU.subtract)
                if u.layer == 1:
                    nc.vector.tensor_copy(s0[1][:, :], kv[:, SO:SO + H])
                    return
                nc.vector.tensor_tensor(s0[0][:, :], kv[:, SO:SO + H], null_bias[0][:, :], ALU.add)
                nc.vector.tensor_copy(k_dup[:, :, :], kv[:, KO:KO + DH].unsqueeze(1).to_broadcast([P, 2, DH])).then_inc(k_ready, 1)
                nc.vector.tensor_copy(q_sb[:, Q2:INNER], kv[:, 0:INNER - Q2]).then_inc(q_ready[2], 1)

            def norms(b):
                def stage(u):
                    lo, hi = QH[b]
                    wait(dve, q_squared[b], u.sdone)
                    nc.vector.tensor_reduce(norm_sq[:, lo:hi], q_sb[:, lo * DH:hi * DH].rearrange("p (h d) -> p h d", d=DH),
                                            AX.X, ALU.add).then_inc(norm_summed[b], 1)
                    wait(dve, norm_summed[b], u.sdone)
                    hi += (b == 2)
                    nc.vector.tensor_scalar(norm_sq[:, lo:hi], norm_sq[:, lo:hi], NORM_FLOOR, None,
                                            ALU.max).then_inc(norm_floored[b], 1)
                return stage

            def unit_q(b):
                def stage(u):
                    lo, hi = QH[b]
                    wait(dve, norm_inv_done[b], u.sdone)
                    if b == 2:
                        nc.vector.tensor_scalar(k_dup[:, :, :], Q[2][:, KO:KO + DH].unsqueeze(1).to_broadcast([P, 2, DH]),
                                                norm_inv[:, H:H + 1], None, ALU.mult).then_inc(k_ready, 1)
                    nc.vector.tensor_tensor(q_sb[:, lo * DH:hi * DH].rearrange("p (h d) -> p h d", d=DH),
                                            Q[b][:, 0:(hi - lo) * DH].rearrange("p (h d) -> p h d", d=DH),
                                            norm_inv[:, lo:hi].unsqueeze(2).to_broadcast([P, hi - lo, DH]),
                                            ALU.mult).then_inc(q_ready[b], 1)
                return stage

            def unit_s0(u):
                nc.vector.tensor_tensor(s0[1][:, :], s0[1][:, :], norm_inv[:, 0:H], ALU.mult).then_inc(s0_scaled, 1)
                wait(dve, s0_scaled, u.sdone)
                nc.vector.tensor_tensor(s0[1][:, :], s0[1][:, :], null_bias[1][:, :], ALU.add).then_inc(s0_done, 1)

            def take_kt(u):
                wait(dve, kt_done, u.done)
                nc.vector.tensor_scalar(k_diag[0:DH, 0:S], Q[2][0:DH, 0:S], k_scale[u.layer][0:DH, 0:1], None, ALU.mult)
                nc.vector.tensor_scalar(k_diag[DH:P, S:2 * S], Q[2][DH:P, 0:S], k_scale[u.layer][DH:P, 0:1], None,
                                        ALU.mult).then_inc(k_diag_done, 1)

            def softmax(u, between=(None, None, None)):
                def add_bias(c):
                    wait(dve, scores_done[c], u.done)
                    nc.vector.tensor_tensor(probs[:, c * CH:(c + 1) * CH, 0:S], SP[c % 2].rearrange("p (h s) -> p h s", h=CH),
                                            masked_bias[:, c * CH:(c + 1) * CH, :], ALU.add).then_inc(biased[c], 1)

                def row_max(c):
                    wait(dve, biased[c], u.done)
                    nc.vector.tensor_reduce(neg_max[:, c * CH:(c + 1) * CH], probs[:, c * CH:(c + 1) * CH, :], AX.X, ALU.max,
                                            negate=True).then_inc(max_done[c], 1)

                def inverse(c):
                    wait(dve, exp_done[c], u.done)
                    nc.vector.reciprocal(den_inv[:, c * CH:(c + 1) * CH], den[:, c * CH:(c + 1) * CH]).then_inc(den_inv_done[c], 1)

                wait(dve, scores_done[0], u.done)
                if u.layer == 1:
                    wait(dve, s0_done, u.sdone)
                nc.vector.tensor_copy(probs[:, :, S:S + 1], s0[u.layer][:, :].unsqueeze(2)).then_inc(s0_placed, 1)
                wait(dve, masked_bias_done, u.done)
                add_bias(0)
                wait(dve, s0_placed, u.done)
                row_max(0)
                add_bias(1)
                if between[0]:
                    between[0]()
                add_bias(2)
                row_max(1)
                if between[1]:
                    between[1]()
                add_bias(3)
                row_max(2)
                inverse(0)
                row_max(3)
                inverse(1)
                if between[2]:
                    between[2]()
                inverse(2)
                inverse(3)

            def split_o(u, halves=(0, 1)):
                for g in halves:
                    wait(dve, o_hi_done[g], u.done)
                    nc.vector.scalar_tensor_tensor(o_lo[:, g * 512:(g + 1) * 512], O[g], null_v_col[:, 0:1],
                                                   o_hi[:, g * 512:(g + 1) * 512].bitcast(F32), ALU.add,
                                                   ALU.subtract).then_inc(o_lo_done[g], 1)

            def finish(u):
                dst, res = (x1, x_res) if u.layer == 0 else (x_out, x1_res)
                wait(dve, y_done, u.done)
                nc.vector.bn_stats(bn_out[:, :], Y[:, 0:D]).then_inc(bn_out_done, 1)
                wait_apart(dve, bn_out_done, u.done, dve_passed)
                nc.vector.bn_aggr(mv_out[:, :], bn_out[:, :]).then_inc(mv_out_done, 1)
                wait(dve, mv_out_done, u.done)
                if u.layer == 0:
                    wait(dve, x1_copied, u.same * 16)
                else:
                    wait(dve, out_stored, u.same * 16)
                nc.vector.scalar_tensor_tensor(dst[:, :], Y[:, 0:D], mv_out[:, 0:1], g_out[u.layer][:, :], ALU.subtract,
                                               ALU.mult).then_inc(y_read, 1)
                wait(dve, rstd_out_done, u.done)
                wait(dve, y_read, u.done)
                wait(dve, x_res_loaded if u.layer == 0 else x1_copied, u.sdone * 16)
                nc.vector.scalar_tensor_tensor(dst[:, :], dst[:, :], rstd_out[:, 0:1], res[:, :], ALU.mult,
                                               ALU.add).then_inc(layer_done[u.layer], 1)

            def body(a, a_prev, a_next, b_old, b_new):
                run_stages((split_x, a), (softmax, b_old), (finish, a_prev), (input_statistics, b_new), (take_kv, a),
                           (normalise, b_new), (take_kt, a))
                others = (lambda: run_stages((lambda u: split_o(u, (0,)), b_old)),
                          lambda: run_stages((lambda u: split_o(u, (1,)), b_old)),
                          lambda: run_stages((split_x, b_new)))
                if a:
                    softmax(a, others)
                else:
                    for other in others:
                        other()
                run_stages((finish, b_old), (input_statistics, a_next), (take_kv, b_new), (norms(2), b_new),
                           (unit_q(2), b_new), (norms(0), b_new), (unit_q(0), b_new), (normalise, a_next), (norms(1), b_new),
                           (unit_q(1), b_new), (split_o, a), (unit_s0, b_new), (take_kt, b_new))

            run_units(dve, body, NB)

        @block.gpsimd
        def _(pool):
            def mask_bias(u):
                wait(pool, keep_loaded[u.layer], u.sdone * 16)
                wait_apart(pool, masked_bias_done, u.prev, pool_passed)
                nc.gpsimd.tensor_scalar(pad_neg[:, :], keep[u.layer][:, :], -NEG, NEG, ALU.mult, ALU.add).then_inc(pad_neg_done, 1)
                wait(pool, biased[NCH - 1], u.prev)
                wait(pool, pad_neg_done, u.done)
                nc.gpsimd.tensor_tensor(masked_bias[:, :, :], bias[u.layer][:, :, :],
                                        pad_neg[:, :].unsqueeze(1).to_broadcast([P, H, S]), ALU.add).then_inc(masked_bias_done, 1)

            def divide(u):
                for c in range(NCH):
                    wait(pool, den_inv_done[c], u.done)
                    nc.gpsimd.tensor_tensor(probs[:, c * CH:(c + 1) * CH, 0:S], probs[:, c * CH:(c + 1) * CH, 0:S],
                                            den_inv[:, c * CH:(c + 1) * CH].unsqueeze(2).to_broadcast([P, CH, S]),
                                            ALU.mult).then_inc(probs_done[c], 1)

            def body(a, a_prev, a_next, b_old, b_new):
                run_stages((divide, b_old), (mask_bias, a), (divide, a), (mask_bias, b_new))

            run_units(pool, body, NB)


def setup(nc, ctx, null_kv, bias0, L0, L1, v):
    KC, COLS, INNER, DH, H, D, S, PAIRS = (v[n] for n in ("KC", "COLS", "INNER", "DH", "H", "D", "S", "PAIRS"))
    w_hi, w_lo, wo_hi, wo_lo, bias, g_out, null_bias, k_scale = (
        v[n] for n in ("w_hi", "w_lo", "wo_hi", "wo_lo", "bias", "g_out", "null_bias", "k_scale"))
    null_v, null_v_col, ident, eps_col, root_col, k_diag, psum = (
        v[n] for n in ("null_v", "null_v_col", "ident", "eps_col", "root_col", "k_diag", "psum"))
    layers = (L0, L1)
    diagonals = nc.dram_tensor("diagonals", [H, 2 * S], F32, kind="Internal").ap()

    def row(ap, n):
        return ap.unsqueeze(0).to_broadcast([P, n])

    with ExitStack() as scratch:
        def sb(name, shape, dt=F32):
            return scratch.enter_context(nc.sbuf_tensor(name, shape, dt))

        def sem(name):
            return ctx.enter_context(nc.semaphore(name))

        raw = sb("raw", [P, 2, COLS])
        prod = sb("prod", [P, INNER])
        g_in = [sb(f"g_in{n}", [P, KC]) for n in range(2)]
        null_k = sb("null_k", [P, DH])
        null_k_unit = sb("null_k_unit", [P, DH])
        null_key = [sb(f"null_key{n}", [P, DH]) for n in range(2)]
        scale_row = sb("scale_row", [P, 2, DH])
        scale_col = sb("scale_col", [P, 2])
        nk_sq = sb("nk_sq", [P, DH])
        nk = sb("nk", [P, 4])
        rows = sb("rows", [P, 6, D])
        h = sb("h", [P, D])
        sig = sb("sig", [P, D])
        h_t = sb("h_t", [P, D])
        w1 = sb("w1", [P, KC, D])
        w2 = sb("w2", [P, KC, H])
        b2 = sb("b2", [P, H])
        bn = sb("bn", [P, 6])
        mv = sb("mv", [P, 2])
        rs = sb("rs", [P, 2])
        pos = sb("pos", [P, 1])
        neg_tile = sb("neg_tile", [H, S])
        flip = sb("flip", [P, P])
        diag_sb = sb("diag_sb", [P, H])
        diag_t = sb("diag_t", [H, S])

        small_loaded, mlp_loaded = sem("small_loaded"), sem("mlp_loaded")
        raw_loaded = [sem(f"raw_loaded{n}") for n in range(2)]
        raw_read, hi_done = sem("raw_read"), sem("hi_done")
        ident_zero, ident_done, flip_done = sem("ident_zero"), sem("ident_done"), sem("flip_done")
        pool_done, causal_done = sem("pool_done"), sem("causal_done")
        dve_step, act_step, pe_step = sem("dve_step"), sem("act_step"), sem("pe_step")
        diag_stored, diag_loaded = sem("diag_stored"), sem("diag_loaded")

        small = []
        for n, L in enumerate(layers):
            small += [(g_in[n][:, :], L["g_in"].rearrange("(c p) -> p c", p=P)), (g_out[n][:, :], row(L["g_out"], D)),
                      (null_bias[n][:, :], row(L["null_bias"], H))]
        small += [(null_k[:, :], row(null_kv[0], DH)), (null_v[:, :], row(null_kv[1], DH))]
        for e in range(2):
            half = slice(e * DH, (e + 1) * DH)
            small += [(null_v_col[half, :], null_kv[1].unsqueeze(1)), (scale_col[half, 0:1], L1["q_scale"].unsqueeze(1)),
                      (scale_col[half, 1:2], L1["k_scale"].unsqueeze(1))]
        small += [(scale_row[:, 0, :], row(L1["q_scale"], DH)), (scale_row[:, 1, :], row(L1["k_scale"], DH)),
                  (bias[0][:, :, :], bias0.rearrange("h q k -> q h k"))]
        mlp = [(rows[:, n, :], row(L1[k], D)) for n, k in enumerate(("w0", "b0", "g0", "b1", "g1"))]
        mlp += [(w1[:, :, :], L1["w1"].rearrange("(c p) n -> p c n", p=P)), (w2[:, :, :], L1["w2"].rearrange("(c p) n -> p c n", p=P)),
                (b2[:, :], row(L1["b2"], H))]
        pieces = [("in", n, c) for n in range(2) for c in range(KC)] + [("out", n, c) for n in range(2) for c in range(PAIRS // 2)]

        with nc.Block() as block:
            marks = {}
            split_ready, diag_computed, flipped = sem("split_ready"), sem("diag_computed"), sem("flipped")

            def piece_aps(i, kind, n, c):
                if kind == "in":
                    return raw[:, i % 2, :], w_hi[n][:, c, :], w_lo[n][:, c, :]
                flat = lambda t: t[n][:, 2 * c:2 * c + 2, :].rearrange("p a d -> p (a d)")
                return raw[:, i % 2, 0:2 * D], flat(wo_hi), flat(wo_lo)

            @block.vector
            def _(dve):
                V = nc.vector
                count = [0]

                def step(ins, mark=None):
                    ins.then_inc(dve_step, 1)
                    count[0] += 1
                    dve.wait_ge(dve_step, count[0])
                    marks[mark] = count[0]

                step(V.memset(k_diag[:, :], 0.0))
                step(V.memset(eps_col[:, :], EPS))
                step(V.memset(root_col[:, :], LN_NORM_ROOT))
                step(V.memset(k_scale[0][:, :], DH ** -0.5))
                dve.wait_ge(small_loaded, 16 * len(small))
                step(V.scalar_tensor_tensor(k_scale[1][:, :], scale_col[:, 0:1], 8.0, scale_col[:, 1:2], ALU.mult, ALU.mult))
                step(V.tensor_scalar(null_key[0][:, :], null_k[:, :], DH ** -0.5, None, ALU.mult))
                step(V.tensor_tensor(nk_sq[:, :], null_k[:, :], null_k[:, :], ALU.mult))
                step(V.tensor_reduce(nk[:, 0:1], nk_sq[:, :], AX.X, ALU.add))
                step(V.tensor_scalar(nk[:, 1:2], nk[:, 0:1], NORM_FLOOR, None, ALU.max), "null key's norm")
                dve.wait_ge(act_step, 2)
                step(V.tensor_scalar(null_k_unit[:, :], null_k[:, :], nk[:, 3:4], None, ALU.mult))
                step(V.scalar_tensor_tensor(nk_sq[:, :], scale_row[:, 0, :], 8.0, scale_row[:, 1, :], ALU.mult, ALU.mult))
                step(V.tensor_tensor(null_key[1][:, :], null_k_unit[:, :], nk_sq[:, :], ALU.mult))

                dve.wait_ge(mlp_loaded, 16 * len(mlp))
                dve.wait_ge(pool_done, 2)
                step(V.tensor_scalar(h[:, :], rows[:, 0, :], pos[:, 0:1], None, ALU.mult))
                step(V.tensor_tensor(h[:, :], h[:, :], rows[:, 1, :], ALU.add))

                def norm_silu(layer, gain):
                    step(V.bn_stats(bn[:, :], h[:, :]))
                    step(V.bn_aggr(mv[:, :], bn[:, :]), f"statistics {layer}")
                    step(V.scalar_tensor_tensor(h[:, :], h[:, :], mv[:, 0:1], gain, ALU.subtract, ALU.mult))
                    dve.wait_ge(act_step, 4 + 3 * layer)
                    step(V.tensor_scalar(h[:, :], h[:, :], rs[:, 1:2], None, ALU.mult), f"normed {layer}")
                    dve.wait_ge(act_step, 5 + 3 * layer)
                    step(V.tensor_scalar(sig[:, :], sig[:, :], 1.0, None, ALU.add))
                    step(V.reciprocal(sig[:, :], sig[:, :]))
                    step(V.tensor_tensor(h[:, :], h[:, :], sig[:, :], ALU.mult), f"silu {layer}")

                norm_silu(0, rows[:, 2, :])
                dve.wait_ge(pe_step, 1)
                step(V.tensor_copy(h_t[:, :], psum[:, 0, :]), "silu^T 0")
                dve.wait_ge(pe_step, 2)
                step(V.tensor_tensor(h[:, :], psum[:, 1, :], rows[:, 3, :], ALU.add))
                norm_silu(1, rows[:, 4, :])
                dve.wait_ge(pe_step, 3)
                step(V.tensor_copy(h_t[:, :], psum[:, 0, :]), "silu^T 1")
                dve.wait_ge(pe_step, 4)
                step(V.tensor_tensor(diag_sb[:, :], psum[:, 1, 0:H], b2[:, :], ALU.add), "diagonals")
                dve.wait_ge(pe_step, 5)
                V.tensor_copy(diag_t[:, :], psum[0:H, 2, 0:S]).then_inc(diag_computed, 1)

                for i, (kind, n, c) in enumerate(pieces):
                    dve.wait_ge(raw_loaded[i % 2], 32 * (i // 2 + 1))
                    src, hi, lo = piece_aps(i, kind, n, c)
                    w = raw[:, i % 2, :]
                    if kind == "in":
                        step(V.tensor_scalar(w[:, 0:INNER + 2 * DH], w[:, 0:INNER + 2 * DH], g_in[n][:, c:c + 1], None, ALU.mult))
                        step(V.tensor_tensor(prod[:, :].rearrange("p (h d) -> p h d", d=DH), w[:, 0:INNER].rearrange("p (h d) -> p h d", d=DH),
                                             null_key[n][:, :].unsqueeze(1).to_broadcast([P, H, DH]), ALU.mult))
                        step(V.tensor_reduce(w[:, INNER + 2 * DH:COLS], prod[:, :].rearrange("p (h d) -> p h d", d=DH), AX.X, ALU.add))
                    V.engine_nop().then_inc(split_ready, 1)
                    dve.wait_ge(hi_done, i + 1)
                    V.tensor_tensor(lo, src, hi.bitcast(F32), ALU.subtract).then_inc(raw_read, 1)
                dve.wait_ge(raw_read, len(pieces))

            @block.sync
            def _(sp):
                for dst, src in small:
                    sp.dma_start(dst, src, allow_slow_non_contiguous=True).then_inc(small_loaded, 16)
                for i, (kind, n, c) in enumerate(pieces):
                    if i >= 2:
                        sp.wait_ge(raw_read, i - 1)
                    L, slot = layers[n], i % 2
                    if kind == "in":
                        sp.dma_start(raw[:, slot, 0:INNER], L["Wq"][c * P:(c + 1) * P, :]).then_inc(raw_loaded[slot], 16)
                        sp.dma_start(raw[:, slot, INNER:INNER + 2 * DH], L["Wkv"][c * P:(c + 1) * P, :]).then_inc(raw_loaded[slot], 16)
                    else:
                        for k in range(2):
                            j = 2 * c + k
                            sp.dma_start(raw[:, slot, k * D:(k + 1) * D], L["Wo"][j * P:(j + 1) * P, :]).then_inc(raw_loaded[slot], 16)

            @block.scalar
            def _(act):
                act.preload_act_table_set("natural_log_exp_and_others")
                for dst, src in mlp:
                    act.dma_start(dst, src).then_inc(mlp_loaded, 16)
                count = [0]

                def step(need, ins_of):
                    act.wait_ge(dve_step, marks[need])
                    ins_of().then_inc(act_step, 1)
                    count[0] += 1
                    act.wait_ge(act_step, count[0])

                step("null key's norm", lambda: nc.scalar.activation(nk[:, 2:3], nk[:, 1:2], ACT.Ln, scale=NORM_SCALE))
                step("null key's norm", lambda: nc.scalar.activation(nk[:, 3:4], nk[:, 2:3], ACT.Exp, scale=-0.5, bias=root_col[:, 0:1]))
                for layer in range(2):
                    step(f"statistics {layer}", lambda: nc.scalar.activation(rs[:, 0:1], mv[:, 1:2], ACT.Ln, bias=eps_col[:, 0:1]))
                    step(f"statistics {layer}", lambda: nc.scalar.activation(rs[:, 1:2], rs[:, 0:1], ACT.Exp, scale=-0.5))
                    step(f"normed {layer}", lambda: nc.scalar.activation(sig[:, :], h[:, :], ACT.Exp, scale=-1.0))
                for i, (kind, n, c) in enumerate(pieces):
                    act.wait_ge(split_ready, i + 1)
                    src, hi, _ = piece_aps(i, kind, n, c)
                    nc.scalar.copy(hi, src).then_inc(hi_done, 1)
                act.wait_ge(diag_computed, 1)
                act.dma_start(diagonals[:, 0:S], diag_t[:, :]).then_inc(diag_stored, 16)
                act.dma_start(diagonals[:, S:2 * S], neg_tile[:, :]).then_inc(diag_stored, 16)
                act.wait_ge(diag_stored, 32)
                act.dma_start(bias[1][:, :, :], bass.AP(diagonals.tensor, 0, [[1, P], [2 * S, H], [1, S]])).then_inc(diag_loaded, 16)
                for c in range(4):
                    act.wait_ge(flipped, c + 1)
                    nc.scalar.copy(bias[1][:, 4 * c:4 * c + 4, :], psum[:, 3 + c, :].rearrange("p (h s) -> p h s", h=4))

            @block.gpsimd
            def _(pool):
                nc.gpsimd.memset(ident[:, :], 0.0).then_inc(ident_zero, 1)
                pool.wait_ge(ident_zero, 1)
                nc.gpsimd.affine_select(out=ident[:, :], in_=ident[:, :], compare_op=ALU.not_equal, fill=1.0, base=0,
                                        pattern=[[-1, P]], channel_multiplier=1).then_inc(ident_done, 1)
                nc.gpsimd.memset(flip[:, :], 0.0).then_inc(ident_zero, 1)
                pool.wait_ge(ident_zero, 2)
                nc.gpsimd.affine_select(out=flip[:, :], in_=flip[:, :], compare_op=ALU.not_equal, fill=1.0, base=1 - S,
                                        pattern=[[1, P]], channel_multiplier=1).then_inc(flip_done, 1)
                nc.gpsimd.iota(pos[:, :], pattern=[[0, 1]], base=S - 1, channel_multiplier=-1,
                               allow_small_or_imprecise_dtypes=True).then_inc(pool_done, 1)
                nc.gpsimd.memset(neg_tile[:, :], NEG).then_inc(pool_done, 1)
                pool.wait_ge(small_loaded, 16 * len(small))
                nc.gpsimd.affine_select(out=bias[0][:, :, :], in_=bias[0][:, :, :], compare_op=ALU.is_ge, fill=NEG, base=0,
                                        pattern=[[0, H], [-1, S]], channel_multiplier=1).then_inc(causal_done, 1)
                pool.wait_ge(causal_done, 1)

            @block.tensor
            def _(pe):
                pe.wait_ge(ident_done, 1)

                def transposed_h(layer):
                    pe.wait_ge(dve_step, marks[f"silu {layer}"])
                    for c in range(KC):
                        t = nc.tensor.transpose(psum[:, 0, c * P:(c + 1) * P], h[:, c * P:(c + 1) * P], ident[:, :])
                    t.then_inc(pe_step, 1)

                transposed_h(0)
                pe.wait_ge(dve_step, marks["silu^T 0"])
                for c in range(KC):
                    m = nc.tensor.matmul(psum[:, 1, :], h_t[:, c * P:(c + 1) * P], w1[:, c, :], start=(c == 0), stop=(c == KC - 1))
                m.then_inc(pe_step, 1)
                transposed_h(1)
                pe.wait_ge(dve_step, marks["silu^T 1"])
                for c in range(KC):
                    m = nc.tensor.matmul(psum[:, 1, 0:H], h_t[:, c * P:(c + 1) * P], w2[:, c, :], start=(c == 0), stop=(c == KC - 1))
                m.then_inc(pe_step, 1)
                pe.wait_ge(dve_step, marks["diagonals"])
                nc.tensor.transpose(psum[0:H, 2, 0:S], diag_sb[:, :], ident[:, :]).then_inc(pe_step, 1)
                pe.wait_ge(flip_done, 1)
                pe.wait_ge(diag_loaded, 16)
                for c in range(4):
                    nc.tensor.matmul(psum[:, 3 + c, :], flip[:, :], bias[1][:, 4 * c:4 * c + 4, :].rearrange("p h s -> p (h s)"),
                                     start=True, stop=True).then_inc(flipped, 1)


_COMMON = ["x", "fside_16xSxS_0", "cond_64", "mask_BxS_bk0", "mask_BxS_bf1"]
_L0 = {"g_in": "g_in", "null_bias": "null_attn_bias", "Wq": "Wq", "Wkv": "Wkv", "Wo": "Wo", "g_out": "g_out"}
_L1 = {"g_in": "g_norm", "null_bias": "null_attn_bias", "Wq": "Wq", "Wkv": "Wkv", "Wo": "Wout", "g_out": "g_out",
       "q_scale": "q_scale", "k_scale": "k_scale", "w0": "w0", "b0": "b0", "g0": "g0", "w1": "w1", "b1": "b1", "g1": "g1",
       "w2": "w2", "b2": "b2"}


def kernel(**inputs):
    import numpy as _np
    import concourse.bacc as _bacc
    from concourse import mybir as _mybir
    from concourse.bass_utils import run_bass_kernel_spmd as _run

    nc = _bacc.Bacc("TRN2", target_bir_lowering=False, num_devices=1,
                    dynamic_dma_scratch_size=1024)
    arrays = {}

    def give(name):
        a = _np.ascontiguousarray(inputs[name])
        if name == "L1_cond_w0":
            a = a.reshape(-1)
        arrays[f"in_{name}_dram"] = a
        return nc.dram_tensor(f"in_{name}_dram", a.shape, _mybir.dt.from_np(a.dtype), kind="ExternalInput").ap()

    x, bias0, null_kv, keep0, keep1 = (give(n) for n in _COMMON)
    L0 = {k: give("L0_cond_" + n) for k, n in _L0.items()}
    L1 = {k: give("L1_cond_" + n) for k, n in _L1.items()}
    out = nc.dram_tensor("out_0_dram", inputs["x"].shape, F32, kind="ExternalOutput").ap()
    build(nc, x, bias0, null_kv, keep0, keep1, L0, L1, out)
    r = _run(nc, [arrays], core_ids=[0])
    return r.results[0]["out_0_dram"]
```

```python
from contextlib import ExitStack

import concourse.bass as bass
from concourse import mybir

F32 = mybir.dt.float32
F32R = mybir.dt.float32r
U8 = mybir.dt.uint8
ALU = mybir.AluOpType
ACT = mybir.ActivationFunctionType
AX = mybir.AxisListType

P = 128
EPS = 1e-5
NEG = -1e38
NORM_FLOOR = 1e-24
NORM_SCALE = 2.0 ** 16
LN_NORM_ROOT = 8 * 0.6931471805599453


class Unit:

    def __init__(self, layer, batch, done, prev, same, sdone):
        self.layer, self.batch, self.done, self.prev, self.same, self.sdone = layer, batch, done, prev, same, sdone


def static_unit(layer, batch, nb):
    if layer == 0:
        u = 0 if batch == 0 else 2 * batch - 1
    else:
        u = 2 * batch + 2 if batch < nb - 1 else 2 * nb - 1
    return Unit(layer, batch, u + 1, u, batch, batch + 1)


def wait(eng, sem, value):
    if isinstance(value, int) and value <= 0:
        return
    eng.wait_ge(sem, value)


def wait_apart(eng, sem, value, passed):
    if not isinstance(value, int):
        eng.wait_ge(sem, value)
        eng.sem_inc(passed, 1)
    else:
        wait(eng, sem, value)


def run_units(eng, body, nb):
    A = lambda a: static_unit(0, a, nb)
    B = lambda b: static_unit(1, b, nb)
    body(None, None, A(0), None, None)
    body(A(0), None, A(1), None, None)
    body(A(1), A(0), A(2), None, B(0))
    body(A(2), A(1), A(3), B(0), B(1))
    with eng.Fori(3, nb - 1) as i:
        twice = {k: eng.snap(i * 2 + k) for k in range(-3, 3)}
        once = {k: eng.snap(i + k) for k in (-2, -1, 1, 2)}
        once[0] = i
        a, a_prev, a_next = (Unit(0, once[k], twice[2 * k], twice[2 * k - 1], once[k], once[k + 1]) for k in (0, -1, 1))
        b_old = Unit(1, once[-2], twice[-1], twice[-2], once[-2], once[-1])
        b_new = Unit(1, once[-1], twice[1], twice[0], once[-1], once[0])
        body(a, a_prev, a_next, b_old, b_new)
    body(A(nb - 1), A(nb - 2), None, B(nb - 3), B(nb - 2))
    body(None, A(nb - 1), None, B(nb - 2), B(nb - 1))
    body(None, None, None, B(nb - 1), None)


def run_stages(*stages):
    for stage, u in stages:
        if u:
            stage(u)


def row(ap, n):
    return ap.unsqueeze(0).to_broadcast([P, n])


def part(stage, *args):
    return lambda u: stage(u, *args)


def build(nc, x, bias0, null_kv, keep0, keep1, L0, L1, out):
    NB, S, D = x.shape
    H = bias0.shape[0]
    INNER = L0["Wq"].shape[1]
    DH = INNER // H
    KC = D // P
    PAIRS = H // 2
    COLS = INNER + 2 * DH + H
    HG = 6
    QB = [(0, HG * DH), (HG * DH, 2 * HG * DH), (2 * HG * DH, COLS)]
    QH = [(0, HG), (HG, 2 * HG), (2 * HG, H)]
    Q2 = 2 * HG * DH
    KO, VO, SO = INNER - Q2, INNER - Q2 + DH, INNER - Q2 + 2 * DH
    CH = 4
    NCH = H // CH
    assert S == P and DH == 64 and COLS - Q2 <= 512 and D == 512

    ctx = ExitStack()
    with ctx:
        def sb(name, shape, dt=F32, where=ctx):
            return where.enter_context(nc.sbuf_tensor(name, shape, dt))

        def sem(name):
            return ctx.enter_context(nc.semaphore(name))

        psum = ctx.enter_context(nc.psum_tensor("psum", [P, 8, 512], F32))
        Q = [psum[:, b, :] for b in range(3)]
        SP = [psum[:, 3 + b, :] for b in range(2)]
        O = [psum[:, 5 + b, :] for b in range(2)]
        Y = psum[:, 7, :]

        w_hi = [sb(f"w_hi{n}", [P, KC, COLS], F32R) for n in range(2)]
        w_lo = [sb(f"w_lo{n}", [P, KC, COLS], F32R) for n in range(2)]
        wo_hi = [sb(f"wo_hi{n}", [P, PAIRS, D], F32R) for n in range(2)]
        wo_lo = [sb(f"wo_lo{n}", [P, PAIRS, D], F32R) for n in range(2)]
        bias = [sb(f"bias{n}", [P, H, S]) for n in range(2)]
        g_out = [sb(f"g_out{n}", [P, D]) for n in range(2)]
        null_bias = [sb(f"null_bias{n}", [P, H]) for n in range(2)]
        k_scale = [sb(f"k_scale{n}", [P, 1]) for n in range(2)]
        null_v = sb("null_v", [P, DH])
        null_v_col = sb("null_v_col", [P, 1])
        ident = sb("ident", [P, P])
        eps_col = sb("eps_col", [P, 1])
        root_col = sb("root_col", [P, 1])
        k_hi = sb("k_hi", [P, 2 * S], F32R)
        k_lo = sb("k_lo", [P, 2 * S], F32R)

        xa = sb("xa", [P, D])
        keep = [sb(f"keep{n}", [P, S], U8) for n in range(2)]
        xa_loaded = sem("xa_loaded")
        keep_loaded = [sem(f"keep_loaded{n}") for n in range(2)]
        first_loads = [(xa[:, :], x[0], xa_loaded), (keep[0][:, :], row(keep0[0], S), keep_loaded[0]),
                       (keep[1][:, :], row(keep1[0], S), keep_loaded[1])]
        setup(nc, ctx, null_kv, bias0, L0, L1, first_loads, dict(
            KC=KC, COLS=COLS, INNER=INNER, DH=DH, H=H, D=D, S=S, PAIRS=PAIRS, w_hi=w_hi, w_lo=w_lo, wo_hi=wo_hi, wo_lo=wo_lo,
            bias=bias, g_out=g_out, null_bias=null_bias, k_scale=k_scale, null_v=null_v, null_v_col=null_v_col, ident=ident,
            eps_col=eps_col, root_col=root_col, k_hi=k_hi, k_lo=k_lo, psum=psum))

        x_res = sb("x_res", [P, D])
        x1 = sb("x1", [P, D])
        x1_res = sb("x1_res", [P, D])
        x_out = sb("x_out", [P, D])
        xn = sb("xn", [P, D])
        x_hi = sb("x_hi", [P, D], F32R)
        x_lo = sb("x_lo", [P, D], F32R)
        q_sb = sb("q_sb", [P, INNER])
        q_hi = sb("q_hi", [P, INNER], F32R)
        q_lo = sb("q_lo", [P, INNER], F32R)
        k_dup = sb("k_dup", [P, 2, DH])
        v_diff = [sb(f"v_diff{n}", [P, DH]) for n in range(2)]
        s0 = [sb(f"s0_{n}", [P, H]) for n in range(2)]
        masked_bias = sb("masked_bias", [P, H, S])
        pad_neg = sb("pad_neg", [P, S])
        probs = sb("probs", [P, H, S + 1])
        o_hi = sb("o_hi", [P, PAIRS * P], F32R)
        o_lo = sb("o_lo", [P, PAIRS * P], F32R)
        bn_in = sb("bn_in", [P, 6])
        mv_in = sb("mv_in", [P, 2])
        rstd_in = sb("rstd_in", [P, 1])
        ln_in = sb("ln_in", [P, 1])
        bn_out = sb("bn_out", [P, 6])
        mv_out = sb("mv_out", [P, 2])
        rstd_out = sb("rstd_out", [P, 1])
        ln_out = sb("ln_out", [P, 1])
        norm_sq = sb("norm_sq", [P, H + 1])
        norm_ln = sb("norm_ln", [P, H + 1])
        norm_inv = sb("norm_inv", [P, H + 1])
        neg_max = sb("neg_max", [P, H])
        den = sb("den", [P, H])
        den_inv = sb("den_inv", [P, H])

        x_res_loaded = sem("x_res_loaded")
        x1_copied, out_stored = sem("x1_copied"), sem("out_stored")
        bn_in_done, mv_in_done, ln_in_done, rstd_in_done = (sem(n) for n in ("bn_in_done", "mv_in_done", "ln_in_done", "rstd_in_done"))
        xn_done, xt_done, x_hi_done, x_lo_done = (sem(n) for n in ("xn_done", "xt_done", "x_hi_done", "x_lo_done"))
        proj_done = [sem(f"proj_done{n}") for n in range(3)]
        q_ready = [sem(f"q_ready{n}") for n in range(3)]
        q_squared = [sem(f"q_squared{n}") for n in range(3)]
        norm_summed = [sem(f"norm_summed{n}") for n in range(3)]
        norm_floored = [sem(f"norm_floored{n}") for n in range(3)]
        norm_ln_done = [sem(f"norm_ln_done{n}") for n in range(3)]
        norm_inv_done = [sem(f"norm_inv_done{n}") for n in range(3)]
        k_ready, s0_scaled, s0_done = sem("k_ready"), sem("s0_scaled"), sem("s0_done")
        kt_done, k_hi_done, k_lo_done = sem("kt_done"), sem("k_hi_done"), sem("k_lo_done")
        qt_done = [sem(f"qt_done{n}") for n in range(2)]
        q_hi_done = [sem(f"q_hi_done{n}") for n in range(2)]
        q_lo_done = [sem(f"q_lo_done{n}") for n in range(2)]
        pad_neg_done, masked_bias_done = sem("pad_neg_done"), sem("masked_bias_done")
        scores_done = [sem(f"scores_done{n}") for n in range(NCH)]
        s0_placed = sem("s0_placed")
        biased = [sem(f"biased{n}") for n in range(NCH)]
        max_done = [sem(f"max_done{n}") for n in range(NCH)]
        exp_done = [sem(f"exp_done{n}") for n in range(NCH)]
        den_inv_done = [sem(f"den_inv_done{n}") for n in range(NCH)]
        probs_done = [sem(f"probs_done{n}") for n in range(NCH)]
        pt_done = [sem(f"pt_done{n}") for n in range(NCH)]
        pt_copied = [sem(f"pt_copied{n}") for n in range(NCH)]
        values_done = [sem(f"values_done{n}") for n in range(2)]
        o_hi_done = [sem(f"o_hi_done{n}") for n in range(2)]
        o_lo_done = [sem(f"o_lo_done{n}") for n in range(2)]
        y_done, bn_out_done, mv_out_done, ln_out_done, rstd_out_done, y_read = (
            sem(n) for n in ("y_done", "bn_out_done", "mv_out_done", "ln_out_done", "rstd_out_done", "y_read"))
        layer_done = [sem(f"layer_done{n}") for n in range(2)]

        sp_passed, dve_passed, pool_passed = sem("sp_passed"), sem("dve_passed"), sem("pool_passed")

        block = ctx.enter_context(nc.Block())

        @block.sync
        def _(sp):
            def load_xa(batch):
                sp.dma_start(xa[:, :], x[batch]).then_inc(xa_loaded, 16)

            def load_keep(layer, batch):
                src = (keep0, keep1)[layer][batch]
                sp.dma_start(keep[layer][:, :], row(src, S)).then_inc(keep_loaded[layer], 16)

            def body(a, a_prev, a_next, b_old, b_new):
                if a and a_next:
                    wait_apart(sp, xn_done, a.done, sp_passed)
                    load_xa(a.batch + 1)
                if a_prev:
                    wait_apart(sp, layer_done[0], a_prev.sdone, sp_passed)
                if a:
                    sp.dma_start(x_res[:, :], x[a.batch]).then_inc(x_res_loaded, 16)
                if a and a_next:
                    wait_apart(sp, pad_neg_done, a.done, sp_passed)
                    load_keep(0, a.batch + 1)
                if b_old:
                    wait_apart(sp, layer_done[1], b_old.sdone, sp_passed)
                    sp.dma_start(out[b_old.batch], x_out[:, :]).then_inc(out_stored, 16)
                if b_new:
                    sp.dma_start(x1_res[:, :], x1[:, :]).then_inc(x1_copied, 16)
                    if not (isinstance(b_new.batch, int) and b_new.batch == NB - 1):
                        wait_apart(sp, pad_neg_done, b_new.done, sp_passed)
                        load_keep(1, b_new.batch + 1)

            run_units(sp, body, NB)
            sp.wait_ge(out_stored, 16 * NB)

        @block.tensor
        def _(pe):
            def transpose_x(u):
                wait(pe, xn_done, u.done)
                wait(pe, k_lo_done, u.prev)
                for c in range(KC):
                    t = nc.tensor.transpose(Q[2][:, c * P:(c + 1) * P], xn[:, c * P:(c + 1) * P], ident[:, :])
                t.then_inc(xt_done, 1)

            def project(u, banks=(2, 0, 1)):
                wait(pe, x_lo_done, u.done)
                for b in banks:
                    if b < 2:
                        wait(pe, q_lo_done[b], u.prev)
                    lo, hi = QB[b]
                    n = 0
                    for xs, ws in ((x_hi, w_hi), (x_lo, w_hi), (x_hi, w_lo)):
                        for c in range(KC):
                            m = nc.tensor.matmul(Q[b][:, 0:hi - lo], xs[:, c * P:(c + 1) * P], ws[u.layer][:, c, lo:hi],
                                                 start=(n == 0), stop=(n == 3 * KC - 1))
                            n += 1
                    m.then_inc(proj_done[b], 1)

            def transpose_k(u):
                wait(pe, k_ready, u.done)
                wait(pe, q_ready[2], u.done)
                nc.tensor.transpose(Q[2][:, 0:P], k_dup[:, :, :].rearrange("p a d -> p (a d)"), ident[:, :]).then_inc(kt_done, 1)

            def transpose_q(u):
                wait(pe, q_ready[0], u.done)
                wait(pe, q_ready[1], u.done)
                for j in range(PAIRS):
                    t = nc.tensor.transpose(Q[j // 4][:, (j % 4) * P:(j % 4 + 1) * P], q_sb[:, j * P:(j + 1) * P], ident[:, :])
                    if j % 4 == 3:
                        t.then_inc(qt_done[j // 4], 1)

            def scores(u, chunks):
                wait(pe, k_lo_done, u.done)
                for c in chunks:
                    wait(pe, q_lo_done[c // 2], u.done)
                    if c < 2:
                        wait(pe, pt_copied[c + 2], u.prev)
                    else:
                        wait(pe, biased[c - 2], u.done)
                    for jj in range(2):
                        j = 2 * c + jj
                        for n, (qs, ks) in enumerate(((q_hi, k_hi), (q_lo, k_hi), (q_hi, k_lo))):
                            m = nc.tensor.matmul(SP[c % 2][:, jj * 2 * S:(jj + 1) * 2 * S], qs[:, j * P:(j + 1) * P], ks[:, :],
                                                 start=(n == 0), stop=(n == 2))
                    m.then_inc(scores_done[c], 1)

            def transpose_p(u, chunks):
                for c in chunks:
                    wait(pe, probs_done[c], u.done)
                    wait(pe, biased[c + 2] if c < 2 else pt_copied[c - 2], u.done)
                    for h in range(CH):
                        t = nc.tensor.transpose(SP[c % 2][:, h * S:(h + 1) * S], probs[:, c * CH + h, 0:S], ident[:, :])
                    t.then_inc(pt_done[c], 1)

            def values(u):
                for g in range(2):
                    wait(pe, pt_copied[2 * g], u.done)
                    wait(pe, pt_copied[2 * g + 1], u.done)
                    wait(pe, o_lo_done[g], u.prev)
                    for par in range(2):
                        m = nc.tensor.matmul(O[g][par * DH:(par + 1) * DH, :], v_diff[u.layer][:, :],
                                             probs[:, 8 * g + par:8 * g + 8:2, 0:S], start=True, stop=True)
                    m.then_inc(values_done[g], 1)

            def project_out(u, half, passes):
                for p in passes:
                    if p == 0:
                        wait(pe, o_lo_done[half], u.done)
                        if half == 0:
                            wait(pe, y_read, u.prev)
                    os, ws = ((o_hi, wo_hi), (o_lo, wo_hi), (o_hi, wo_lo))[p]
                    for j in range(4 * half, 4 * half + 4):
                        m = nc.tensor.matmul(Y[:, 0:D], os[:, j * P:(j + 1) * P], ws[u.layer][:, j, :],
                                             start=(p == 0 and j == 0), stop=(p == 2 and j == PAIRS - 1))
                if half == 1 and passes[-1] == 2:
                    m.then_inc(y_done, 1)

            def body(a, a_prev, a_next, b_old, b_new):
                run_stages((part(scores, (0, 1)), b_old), (transpose_x, a), (part(project_out, 1, (0,)), a_prev),
                           (part(scores, (2, 3)), b_old), (part(project_out, 1, (1, 2)), a_prev), (project, a),
                           (part(transpose_p, (0, 1)), b_old), (transpose_k, a), (transpose_q, a),
                           (part(transpose_p, (2, 3)), b_old), (values, b_old),
                           (part(scores, (0, 1)), a), (transpose_x, b_new), (part(project_out, 0, (0,)), b_old),
                           (part(scores, (2, 3)), a), (part(project_out, 0, (1, 2)), b_old),
                           (part(project_out, 1, (0, 1, 2)), b_old), (part(project, (2,)), b_new),
                           (part(transpose_p, (0, 1)), a), (part(project, (0, 1)), b_new), (part(transpose_p, (2, 3)), a),
                           (transpose_k, b_new), (values, a), (transpose_q, b_new), (part(project_out, 0, (0, 1, 2)), a))

            run_units(pe, body, NB)

        @block.scalar
        def _(act):
            def root(var, tmp, res, ready, between, finished, u):
                wait(act, ready, u.done)
                nc.scalar.activation(tmp, var, ACT.Ln, bias=eps_col[:, 0:1]).then_inc(between, 1)
                wait(act, between, u.done)
                nc.scalar.activation(res, tmp, ACT.Exp, scale=-0.5).then_inc(finished, 1)

            def rstd_of_input(u):
                root(mv_in[:, 1:2], ln_in[:, :], rstd_in[:, :], mv_in_done, ln_in_done, rstd_in_done, u)

            def rstd_of_output(u):
                root(mv_out[:, 1:2], ln_out[:, :], rstd_out[:, :], mv_out_done, ln_out_done, rstd_out_done, u)

            def split_x(u):
                wait(act, xt_done, u.done)
                nc.scalar.copy(x_hi[:, :], Q[2][:, :]).then_inc(x_hi_done, 1)

            def take_q(u):
                for b in (0, 1):
                    lo, hi = QH[b]
                    wait(act, proj_done[b], u.done)
                    nc.scalar.copy(q_sb[:, lo * DH:hi * DH], Q[b][:, 0:(hi - lo) * DH]).then_inc(q_ready[b], 1)

            def square(b):
                def stage(u):
                    lo, hi = QH[b]
                    wait(act, proj_done[b], u.done)
                    if b == 2:
                        nc.scalar.activation(k_dup[:, 0, :], Q[2][:, KO:KO + DH], ACT.Square,
                                             accum_out=norm_sq[:, H:H + 1])
                    nc.scalar.activation(q_sb[:, lo * DH:hi * DH], Q[b][:, 0:(hi - lo) * DH],
                                         ACT.Square).then_inc(q_squared[b], 1)
                return stage

            def inverse_root(b):
                def stage(u):
                    lo, hi = QH[b]
                    hi += (b == 2)
                    wait(act, norm_floored[b], u.sdone)
                    nc.scalar.activation(norm_ln[:, lo:hi], norm_sq[:, lo:hi], ACT.Ln,
                                         scale=NORM_SCALE).then_inc(norm_ln_done[b], 1)
                    wait(act, norm_ln_done[b], u.sdone)
                    nc.scalar.activation(norm_inv[:, lo:hi], norm_ln[:, lo:hi], ACT.Exp, scale=-0.5,
                                         bias=root_col[:, 0:1]).then_inc(norm_inv_done[b], 1)
                return stage

            def take_qt(u, groups=(0, 1)):
                for g in groups:
                    wait(act, qt_done[g], u.done)
                    nc.scalar.copy(q_hi[:, g * 512:(g + 1) * 512], Q[g][:, :]).then_inc(q_hi_done[g], 1)

            def exponential(u):
                for c in range(NCH):
                    wait(act, max_done[c], u.done)
                    for h in range(c * CH, (c + 1) * CH):
                        e = nc.scalar.activation(probs[:, h, :], probs[:, h, :], ACT.Exp, bias=neg_max[:, h:h + 1],
                                                 accum_out=den[:, h:h + 1])
                    e.then_inc(exp_done[c], 1)

            def take_pt(u, chunks):
                for c in chunks:
                    wait(act, pt_done[c], u.done)
                    nc.scalar.copy(probs[:, c * CH:(c + 1) * CH, 0:S],
                                   SP[c % 2].rearrange("p (h s) -> p h s", h=CH)).then_inc(pt_copied[c], 1)

            def split_o(u):
                for g in range(2):
                    wait(act, values_done[g], u.done)
                    nc.scalar.activation(o_hi[:, g * 512:(g + 1) * 512], O[g], ACT.Identity,
                                         bias=null_v_col[:, 0:1]).then_inc(o_hi_done[g], 1)

            def body(a, a_prev, a_next, b_old, b_new):
                run_stages((split_x, a), (exponential, b_old),
                           (rstd_of_output, a_prev), (take_q, a), (rstd_of_input, b_new), (part(take_pt, (0, 1)), b_old),
                           (part(take_qt, (0,)), a), (part(take_pt, (2, 3)), b_old), (part(take_qt, (1,)), a), (split_o, b_old),
                           (split_x, b_new), (exponential, a), (rstd_of_input, a_next), (rstd_of_output, b_old),
                           (square(2), b_new), (part(take_pt, (0, 1)), a), (inverse_root(2), b_new),
                           (square(0), b_new), (inverse_root(0), b_new), (square(1), b_new),
                           (part(take_pt, (2, 3)), a), (inverse_root(1), b_new), (split_o, a), (take_qt, b_new))

            run_units(act, body, NB)

        @block.vector
        def _(dve):
            def input_statistics(u):
                if u.layer == 0:
                    wait(dve, xa_loaded, u.sdone * 16)
                else:
                    wait(dve, layer_done[0], u.sdone)
                nc.vector.bn_stats(bn_in[:, :], (xa, x1)[u.layer][:, :]).then_inc(bn_in_done, 1)
                wait_apart(dve, bn_in_done, u.done, dve_passed)
                nc.vector.bn_aggr(mv_in[:, :], bn_in[:, :]).then_inc(mv_in_done, 1)

            def normalise(u):
                wait(dve, rstd_in_done, u.done)
                wait(dve, xt_done, u.prev)
                nc.vector.tensor_scalar(xn[:, :], (xa, x1)[u.layer][:, :], mv_in[:, 0:1], rstd_in[:, 0:1], ALU.subtract,
                                        ALU.mult).then_inc(xn_done, 1)

            def split_x(u):
                wait(dve, x_hi_done, u.done)
                nc.vector.tensor_tensor(x_lo[:, :], Q[2][:, :], x_hi[:, :].bitcast(F32), ALU.subtract).then_inc(x_lo_done, 1)

            def take_kv(u):
                kv = Q[2]
                if u.layer == 0:
                    wait(dve, proj_done[2], u.done)
                else:
                    wait(dve, q_squared[2], u.sdone)
                nc.vector.tensor_tensor(v_diff[u.layer][:, :], kv[:, VO:VO + DH], null_v[:, :], ALU.subtract)
                if u.layer == 1:
                    nc.vector.tensor_copy(s0[1][:, :], kv[:, SO:SO + H])
                    return
                nc.vector.tensor_tensor(s0[0][:, :], kv[:, SO:SO + H], null_bias[0][:, :], ALU.add)
                nc.vector.tensor_copy(k_dup[:, :, :], kv[:, KO:KO + DH].unsqueeze(1).to_broadcast([P, 2, DH])).then_inc(k_ready, 1)
                nc.vector.tensor_copy(q_sb[:, Q2:INNER], kv[:, 0:INNER - Q2]).then_inc(q_ready[2], 1)

            def norms(b):
                def stage(u):
                    lo, hi = QH[b]
                    wait(dve, q_squared[b], u.sdone)
                    nc.vector.tensor_reduce(norm_sq[:, lo:hi], q_sb[:, lo * DH:hi * DH].rearrange("p (h d) -> p h d", d=DH),
                                            AX.X, ALU.add).then_inc(norm_summed[b], 1)
                    wait(dve, norm_summed[b], u.sdone)
                    hi += (b == 2)
                    nc.vector.tensor_scalar(norm_sq[:, lo:hi], norm_sq[:, lo:hi], NORM_FLOOR, None,
                                            ALU.max).then_inc(norm_floored[b], 1)
                return stage

            def unit_q(b):
                def stage(u):
                    lo, hi = QH[b]
                    wait(dve, norm_inv_done[b], u.sdone)
                    if b == 2:
                        nc.vector.tensor_scalar(k_dup[:, :, :], Q[2][:, KO:KO + DH].unsqueeze(1).to_broadcast([P, 2, DH]),
                                                norm_inv[:, H:H + 1], None, ALU.mult).then_inc(k_ready, 1)
                    nc.vector.tensor_tensor(q_sb[:, lo * DH:hi * DH].rearrange("p (h d) -> p h d", d=DH),
                                            Q[b][:, 0:(hi - lo) * DH].rearrange("p (h d) -> p h d", d=DH),
                                            norm_inv[:, lo:hi].unsqueeze(2).to_broadcast([P, hi - lo, DH]),
                                            ALU.mult).then_inc(q_ready[b], 1)
                return stage

            def unit_s0(u):
                nc.vector.tensor_tensor(s0[1][:, :], s0[1][:, :], norm_inv[:, 0:H], ALU.mult).then_inc(s0_scaled, 1)
                wait(dve, s0_scaled, u.sdone)
                nc.vector.tensor_tensor(s0[1][:, :], s0[1][:, :], null_bias[1][:, :], ALU.add).then_inc(s0_done, 1)

            def take_kt(u):
                wait(dve, kt_done, u.done)
                for e in range(2):
                    t = nc.vector.tensor_scalar(k_hi[e * DH:(e + 1) * DH, e * S:(e + 1) * S], Q[2][e * DH:(e + 1) * DH, 0:S],
                                                k_scale[u.layer][e * DH:(e + 1) * DH, 0:1], None, ALU.mult)
                t.then_inc(k_hi_done, 1)

            def split_kt(u):
                wait(dve, k_hi_done, u.done)
                for e in range(2):
                    t = nc.vector.scalar_tensor_tensor(
                        k_lo[e * DH:(e + 1) * DH, e * S:(e + 1) * S], Q[2][e * DH:(e + 1) * DH, 0:S],
                        k_scale[u.layer][e * DH:(e + 1) * DH, 0:1],
                        k_hi[e * DH:(e + 1) * DH, e * S:(e + 1) * S].bitcast(F32), ALU.mult, ALU.subtract)
                t.then_inc(k_lo_done, 1)

            def split_qt(u):
                for g in range(2):
                    wait(dve, q_hi_done[g], u.done)
                    nc.vector.tensor_tensor(q_lo[:, g * 512:(g + 1) * 512], Q[g][:, :], q_hi[:, g * 512:(g + 1) * 512].bitcast(F32),
                                            ALU.subtract).then_inc(q_lo_done[g], 1)

            def place_s0(u):
                wait(dve, scores_done[0], u.done)
                if u.layer == 1:
                    wait(dve, s0_done, u.sdone)
                nc.vector.tensor_copy(probs[:, :, S:S + 1], s0[u.layer][:, :].unsqueeze(2)).then_inc(s0_placed, 1)
                wait(dve, masked_bias_done, u.done)

            def add_bias(u, c):
                wait(dve, scores_done[c], u.done)
                nc.vector.tensor_tensor(probs[:, c * CH:(c + 1) * CH, 0:S], SP[c % 2].rearrange("p (h s) -> p h s", h=CH),
                                        masked_bias[:, c * CH:(c + 1) * CH, :], ALU.add).then_inc(biased[c], 1)

            def row_max(u, c):
                wait(dve, s0_placed, u.done)
                wait(dve, biased[c], u.done)
                nc.vector.tensor_reduce(neg_max[:, c * CH:(c + 1) * CH], probs[:, c * CH:(c + 1) * CH, :], AX.X, ALU.max,
                                        negate=True).then_inc(max_done[c], 1)

            def inverse_sum(u, c):
                wait(dve, exp_done[c], u.done)
                nc.vector.reciprocal(den_inv[:, c * CH:(c + 1) * CH], den[:, c * CH:(c + 1) * CH]).then_inc(den_inv_done[c], 1)

            def split_o(u, halves=(0, 1)):
                for g in halves:
                    wait(dve, o_hi_done[g], u.done)
                    nc.vector.scalar_tensor_tensor(o_lo[:, g * 512:(g + 1) * 512], O[g], null_v_col[:, 0:1],
                                                   o_hi[:, g * 512:(g + 1) * 512].bitcast(F32), ALU.add,
                                                   ALU.subtract).then_inc(o_lo_done[g], 1)

            def start_finish(u):
                dst = (x1, x_out)[u.layer]
                wait(dve, y_done, u.done)
                nc.vector.bn_stats(bn_out[:, :], Y[:, 0:D]).then_inc(bn_out_done, 1)
                wait_apart(dve, bn_out_done, u.done, dve_passed)
                nc.vector.bn_aggr(mv_out[:, :], bn_out[:, :]).then_inc(mv_out_done, 1)
                wait(dve, mv_out_done, u.done)
                if u.layer == 0:
                    wait(dve, x1_copied, u.same * 16)
                else:
                    wait(dve, out_stored, u.same * 16)
                nc.vector.scalar_tensor_tensor(dst[:, :], Y[:, 0:D], mv_out[:, 0:1], g_out[u.layer][:, :], ALU.subtract,
                                               ALU.mult).then_inc(y_read, 1)

            def end_finish(u):
                dst, res = (x1, x_res) if u.layer == 0 else (x_out, x1_res)
                wait(dve, rstd_out_done, u.done)
                wait(dve, y_read, u.done)
                wait(dve, x_res_loaded if u.layer == 0 else x1_copied, u.sdone * 16)
                nc.vector.scalar_tensor_tensor(dst[:, :], dst[:, :], rstd_out[:, 0:1], res[:, :], ALU.mult,
                                               ALU.add).then_inc(layer_done[u.layer], 1)

            def body(a, a_prev, a_next, b_old, b_new):
                run_stages((place_s0, b_old), (part(add_bias, 0), b_old), (part(add_bias, 1), b_old), (part(row_max, 0), b_old),
                           (part(add_bias, 2), b_old), (part(row_max, 1), b_old), (split_x, a), (part(add_bias, 3), b_old),
                           (part(row_max, 2), b_old), (part(row_max, 3), b_old), (part(inverse_sum, 0), b_old),
                           (part(inverse_sum, 1), b_old), (start_finish, a_prev), (part(inverse_sum, 2), b_old),
                           (part(inverse_sum, 3), b_old), (take_kv, a), (end_finish, a_prev), (input_statistics, b_new),
                           (normalise, b_new), (take_kt, a), (split_kt, a), (split_qt, a),
                           (part(split_o, (0,)), b_old), (place_s0, a), (part(add_bias, 0), a), (part(add_bias, 1), a),
                           (part(row_max, 0), a), (part(split_o, (1,)), b_old), (part(add_bias, 2), a), (part(row_max, 1), a),
                           (part(add_bias, 3), a), (part(row_max, 2), a), (split_x, b_new), (part(row_max, 3), a),
                           (part(inverse_sum, 0), a), (part(inverse_sum, 1), a), (input_statistics, a_next),
                           (part(inverse_sum, 2), a), (part(inverse_sum, 3), a), (start_finish, b_old), (normalise, a_next),
                           (take_kv, b_new), (norms(2), b_new), (end_finish, b_old),
                           (unit_q(2), b_new), (norms(0), b_new), (unit_q(0), b_new), (norms(1), b_new),
                           (take_kt, b_new), (unit_q(1), b_new), (part(split_o, (0,)), a), (split_kt, b_new),
                           (part(split_o, (1,)), a), (split_qt, b_new), (unit_s0, b_new))

            run_units(dve, body, NB)

        @block.gpsimd
        def _(pool):
            def mask_bias(u):
                wait(pool, keep_loaded[u.layer], u.sdone * 16)
                wait_apart(pool, masked_bias_done, u.prev, pool_passed)
                nc.gpsimd.tensor_scalar(pad_neg[:, :], keep[u.layer][:, :], -NEG, NEG, ALU.mult, ALU.add).then_inc(pad_neg_done, 1)
                wait(pool, biased[NCH - 1], u.prev)
                wait(pool, pad_neg_done, u.done)
                nc.gpsimd.tensor_tensor(masked_bias[:, :, :], bias[u.layer][:, :, :],
                                        pad_neg[:, :].unsqueeze(1).to_broadcast([P, H, S]), ALU.add).then_inc(masked_bias_done, 1)

            def divide(u):
                for c in range(NCH):
                    wait(pool, den_inv_done[c], u.done)
                    nc.gpsimd.tensor_tensor(probs[:, c * CH:(c + 1) * CH, 0:S], probs[:, c * CH:(c + 1) * CH, 0:S],
                                            den_inv[:, c * CH:(c + 1) * CH].unsqueeze(2).to_broadcast([P, CH, S]),
                                            ALU.mult).then_inc(probs_done[c], 1)

            def body(a, a_prev, a_next, b_old, b_new):
                run_stages((divide, b_old), (mask_bias, a), (divide, a), (mask_bias, b_new))

            run_units(pool, body, NB)


def setup(nc, ctx, null_kv, bias0, L0, L1, first_loads, v):
    KC, COLS, INNER, DH, H, D, S, PAIRS = (v[n] for n in ("KC", "COLS", "INNER", "DH", "H", "D", "S", "PAIRS"))
    w_hi, w_lo, wo_hi, wo_lo, bias, g_out, null_bias, k_scale = (
        v[n] for n in ("w_hi", "w_lo", "wo_hi", "wo_lo", "bias", "g_out", "null_bias", "k_scale"))
    null_v, null_v_col, ident, eps_col, root_col, k_hi, k_lo, psum = (
        v[n] for n in ("null_v", "null_v_col", "ident", "eps_col", "root_col", "k_hi", "k_lo", "psum"))
    layers = (L0, L1)
    diagonals = nc.dram_tensor("diagonals", [H, 2 * S], F32, kind="Internal").ap()

    with ExitStack() as scratch:
        def sb(name, shape, dt=F32):
            return scratch.enter_context(nc.sbuf_tensor(name, shape, dt))

        def sem(name):
            return ctx.enter_context(nc.semaphore(name))

        RAW = 7
        raw = sb("raw", [P, RAW, COLS])
        prod = sb("prod", [P, 2, INNER])
        g_in = [sb(f"g_in{n}", [P, KC]) for n in range(2)]
        null_k = sb("null_k", [P, DH])
        null_k_unit = sb("null_k_unit", [P, DH])
        null_key = [sb(f"null_key{n}", [P, DH]) for n in range(2)]
        scale_row = sb("scale_row", [P, 2, DH])
        scale_col = sb("scale_col", [P, 2])
        nk_sq = sb("nk_sq", [P, DH])
        nk = sb("nk", [P, 4])
        rows = sb("rows", [P, 5, D])
        h = sb("h", [P, D])
        sig = sb("sig", [P, D])
        h_t = sb("h_t", [P, D])
        w1 = bias[1].rearrange("p h s -> p (h s)").rearrange("p (c n) -> p c n", n=D)
        w2 = sb("w2", [P, KC, H])
        b2 = sb("b2", [P, H])
        bn = sb("bn", [P, 6])
        mv = sb("mv", [P, 2])
        rs = sb("rs", [P, 2])
        pos = sb("pos", [P, 1])
        neg_tile = sb("neg_tile", [H, S])
        flip = sb("flip", [P, P])
        diag_sb = sb("diag_sb", [P, H])
        diag_t = sb("diag_t", [H, S])

        null_loaded, gain_loaded, rest_loaded, rows_loaded, w1_loaded = (
            sem(n) for n in ("null_loaded", "gain_loaded", "rest_loaded", "rows_loaded", "w1_loaded"))
        raw_loaded = [sem(f"raw_loaded{n}") for n in range(RAW)]
        null_key_done, w0_multiplied, w0_done, hi_done = (sem(n) for n in ("null_key_done", "w0_multiplied", "w0_done", "hi_done"))
        lo_done = {"dve": sem("lo_done_dve"), "pool": sem("lo_done_pool")}
        ident_zero, ident_done, flip_done = sem("ident_zero"), sem("ident_done"), sem("flip_done")
        pos_done, neg_tile_done, causal_done = sem("pos_done"), sem("neg_tile_done"), sem("causal_done")
        dve_step, act_step, pe_step = sem("dve_step"), sem("act_step"), sem("pe_step")
        diag_computed, diag_stored, flipped = (sem(n) for n in ("diag_computed", "diag_stored", "flipped"))
        diag_loaded = [sem(f"diag_loaded{c}") for c in range(4)]

        null_loads = [(null_k[:, :], row(null_kv[0], DH))]
        gain_loads = [(g_in[n][:, :], L["g_in"].rearrange("(c p) -> p c", p=P)) for n, L in enumerate(layers)]
        null_loads += [(scale_row[:, 0, :], row(L1["q_scale"], DH)), (scale_row[:, 1, :], row(L1["k_scale"], DH))]
        rest_loads = [(bias[0][:, :, :], bias0.rearrange("h q k -> q h k")), (null_v[:, :], row(null_kv[1], DH))]
        for n, L in enumerate(layers):
            rest_loads += [(g_out[n][:, :], row(L["g_out"], D)), (null_bias[n][:, :], row(L["null_bias"], H))]
        for e in range(2):
            half = slice(e * DH, (e + 1) * DH)
            rest_loads += [(null_v_col[half, :], null_kv[1].unsqueeze(1)), (scale_col[half, 0:1], L1["q_scale"].unsqueeze(1)),
                           (scale_col[half, 1:2], L1["k_scale"].unsqueeze(1))]
        rows_loads = [(rows[:, n, :], row(L1[k], D)) for n, k in enumerate(("w0", "b0", "g0", "b1", "g1"))]
        w1_loads = [(w1[:, :, :], L1["w1"].rearrange("(c p) n -> p c n", p=P)),
                    (w2[:, :, :], L1["w2"].rearrange("(c p) n -> p c n", p=P)), (b2[:, :], row(L1["b2"], H))]

        pieces = [("in", n, c) for n in range(2) for c in range(KC)] + [("out", n, c) for n in range(2) for c in range(PAIRS // 2)]
        IN = 2 * KC
        lo_engine = ["pool" if kind == "out" and c % 2 else "dve" for kind, n, c in pieces[:-1]] + ["dve"]

        def split_piece(i):
            kind, n, c = pieces[i]
            slot = raw[:, i % RAW, :]
            if kind == "in":
                return slot, slot, w_hi[n][:, c, :], w_lo[n][:, c, :]
            flat = lambda t: t[n][:, 2 * c:2 * c + 2, :].rearrange("p a d -> p (a d)")
            return slot, slot[:, 0:2 * D], flat(wo_hi), flat(wo_lo)

        def wait_piece(eng, i):
            eng.wait_ge(raw_loaded[i % RAW], 32 * (i // RAW + 1))

        def wait_lo(eng, i):
            eng.wait_ge(lo_done[lo_engine[i]], sum(e == lo_engine[i] for e in lo_engine[:i + 1]))

        order = []
        between = [0, 0, 0, 0, 3, 1, 0, 1, 1, 0]
        for phase, count in enumerate(between):
            order += [("piece", None)] * count + [("phase", phase)]
        order += [("piece", None)] * (len(pieces) - sum(between))
        numbers = iter(range(len(pieces)))
        order = [(what, next(numbers) if what == "piece" else k) for what, k in order]

        def start(eng, loads, loaded):
            for dst, src in loads:
                eng.dma_start(dst, src, allow_slow_non_contiguous=True).then_inc(loaded, 16)

        with nc.Block() as block:
            marks = {}

            @block.vector
            def _(dve):
                V = nc.vector
                count = [0]

                def step(ins, mark=None):
                    ins.then_inc(dve_step, 1)
                    count[0] += 1
                    dve.wait_ge(dve_step, count[0])
                    marks[mark] = count[0]

                def sum_w0(i):
                    dve.wait_ge(w0_multiplied, i + 1)
                    V.tensor_reduce(split_piece(i)[0][:, INNER + 2 * DH:COLS], prod[:, i % 2, :].rearrange("p (h d) -> p h d", d=DH),
                                    AX.X, ALU.add).then_inc(w0_done, 1)

                def low_part(i):
                    if lo_engine[i] != "dve":
                        return
                    _, src, hi, lo = split_piece(i)
                    kind, n, c = pieces[i]
                    dve.wait_ge(hi_done, i + 1)
                    if kind == "in":
                        V.scalar_tensor_tensor(lo, src, g_in[n][:, c:c + 1], hi.bitcast(F32), ALU.mult,
                                               ALU.subtract).then_inc(lo_done["dve"], 1)
                    else:
                        V.tensor_tensor(lo, src, hi.bitcast(F32), ALU.subtract).then_inc(lo_done["dve"], 1)

                def statistics(layer, gain):
                    step(V.bn_stats(bn[:, :], h[:, :]))
                    step(V.bn_aggr(mv[:, :], bn[:, :]), f"statistics {layer}")
                    step(V.scalar_tensor_tensor(h[:, :], h[:, :], mv[:, 0:1], gain, ALU.subtract, ALU.mult))

                def first_layer():
                    dve.wait_ge(rows_loaded, 16 * len(rows_loads))
                    dve.wait_ge(pos_done, 1)
                    step(V.scalar_tensor_tensor(h[:, :], rows[:, 0, :], pos[:, 0:1], rows[:, 1, :], ALU.mult, ALU.add))
                    statistics(0, rows[:, 2, :])

                def second_layer():
                    dve.wait_ge(pe_step, 2)
                    step(V.tensor_tensor(h[:, :], psum[:, 1, :], rows[:, 3, :], ALU.add))
                    statistics(1, rows[:, 4, :])

                def normed(layer):
                    dve.wait_ge(act_step, 4 + 3 * layer)
                    step(V.tensor_scalar(h[:, :], h[:, :], rs[:, 1:2], None, ALU.mult), f"normed {layer}")

                def silu(layer):
                    dve.wait_ge(act_step, 5 + 3 * layer)
                    step(V.tensor_scalar(sig[:, :], sig[:, :], 1.0, None, ALU.add))
                    step(V.reciprocal(sig[:, :], sig[:, :]))
                    step(V.tensor_tensor(h[:, :], h[:, :], sig[:, :], ALU.mult), f"silu {layer}")

                def silu_transposed(layer):
                    dve.wait_ge(pe_step, 1 + 2 * layer)
                    step(V.tensor_copy(h_t[:, :], psum[:, 0, :]), f"silu^T {layer}")

                def last_layer():
                    dve.wait_ge(pe_step, 4)
                    step(V.tensor_tensor(diag_sb[:, :], psum[:, 1, 0:H], b2[:, :], ALU.add), "diagonals")

                def diagonals_transposed():
                    dve.wait_ge(pe_step, 5)
                    V.tensor_copy(diag_t[:, :], psum[0:H, 2, 0:S]).then_inc(diag_computed, 1)

                phases = [first_layer, lambda: normed(0), lambda: silu(0), lambda: silu_transposed(0),
                          second_layer, lambda: normed(1), lambda: silu(1), lambda: silu_transposed(1),
                          last_layer, diagonals_transposed]

                step(V.memset(k_hi[:, :].bitcast(F32), 0.0))
                step(V.memset(k_lo[:, :].bitcast(F32), 0.0))
                step(V.memset(eps_col[:, :], EPS))
                step(V.memset(root_col[:, :], LN_NORM_ROOT))
                step(V.memset(k_scale[0][:, :], DH ** -0.5))
                dve.wait_ge(null_loaded, 16 * len(null_loads))
                V.tensor_scalar(null_key[0][:, :], null_k[:, :], DH ** -0.5, None, ALU.mult).then_inc(null_key_done, 1)
                step(V.tensor_tensor(nk_sq[:, :], null_k[:, :], null_k[:, :], ALU.mult))
                step(V.tensor_reduce(nk[:, 0:1], nk_sq[:, :], AX.X, ALU.add))
                step(V.tensor_scalar(nk[:, 1:2], nk[:, 0:1], NORM_FLOOR, None, ALU.max), "null key's norm")
                dve.wait_ge(act_step, 2)
                step(V.tensor_scalar(null_k_unit[:, :], null_k[:, :], nk[:, 3:4], None, ALU.mult))
                step(V.scalar_tensor_tensor(nk_sq[:, :], scale_row[:, 0, :], 8.0, scale_row[:, 1, :], ALU.mult, ALU.mult))
                V.tensor_tensor(null_key[1][:, :], null_k_unit[:, :], nk_sq[:, :], ALU.mult).then_inc(null_key_done, 1)

                for what, k in order:
                    if what == "phase":
                        phases[k]()
                        continue
                    if k < IN:
                        sum_w0(k)
                    if k > 0:
                        low_part(k - 1)
                low_part(len(pieces) - 1)
                dve.wait_ge(rest_loaded, 16 * len(rest_loads))
                step(V.scalar_tensor_tensor(k_scale[1][:, :], scale_col[:, 0:1], 8.0, scale_col[:, 1:2], ALU.mult, ALU.mult))

            @block.sync
            def _(sp):
                start(sp, null_loads, null_loaded)
                for i, (kind, n, c) in enumerate(pieces):
                    if i == 5:
                        start(sp, w1_loads, w1_loaded)
                    if i == IN:
                        start(sp, rest_loads, rest_loaded)
                    if i >= RAW:
                        wait_lo(sp, i - RAW)
                    L, slot, loaded = layers[n], i % RAW, raw_loaded[i % RAW]
                    if kind == "in":
                        sp.dma_start(raw[:, slot, 0:INNER], L["Wq"][c * P:(c + 1) * P, :]).then_inc(loaded, 16)
                        sp.dma_start(raw[:, slot, INNER:INNER + 2 * DH], L["Wkv"][c * P:(c + 1) * P, :]).then_inc(loaded, 16)
                    else:
                        for k in range(2):
                            j = 2 * c + k
                            sp.dma_start(raw[:, slot, k * D:(k + 1) * D], L["Wo"][j * P:(j + 1) * P, :]).then_inc(loaded, 16)
                for dst, src, loaded in first_loads:
                    sp.dma_start(dst, src).then_inc(loaded, 16)

            @block.scalar
            def _(act):
                act.preload_act_table_set("natural_log_exp_and_others")
                start(act, gain_loads, gain_loaded)
                start(act, rows_loads, rows_loaded)
                count = [0]

                def step(need, ins_of):
                    act.wait_ge(dve_step, marks[need])
                    ins_of().then_inc(act_step, 1)
                    count[0] += 1
                    act.wait_ge(act_step, count[0])

                def high_part(i):
                    _, src, hi, _ = split_piece(i)
                    kind, n, c = pieces[i]
                    wait_piece(act, i)
                    if i == 0:
                        act.wait_ge(gain_loaded, 16 * len(gain_loads))
                    if kind == "in":
                        act.wait_ge(w0_done, i + 1)
                        nc.scalar.mul(hi, src, g_in[n][:, c:c + 1]).then_inc(hi_done, 1)
                    else:
                        nc.scalar.copy(hi, src).then_inc(hi_done, 1)

                def rstd(layer):
                    step(f"statistics {layer}", lambda: nc.scalar.activation(rs[:, 0:1], mv[:, 1:2], ACT.Ln, bias=eps_col[:, 0:1]))
                    step(f"statistics {layer}", lambda: nc.scalar.activation(rs[:, 1:2], rs[:, 0:1], ACT.Exp, scale=-0.5))

                def exponential(layer):
                    step(f"normed {layer}", lambda: nc.scalar.activation(sig[:, :], h[:, :], ACT.Exp, scale=-1.0))

                def store_diagonals():
                    act.wait_ge(diag_computed, 1)
                    act.dma_start(diagonals[:, 0:S], diag_t[:, :]).then_inc(diag_stored, 16)
                    act.wait_ge(neg_tile_done, 1)
                    act.dma_start(diagonals[:, S:2 * S], neg_tile[:, :]).then_inc(diag_stored, 16)

                phases = {0: lambda: rstd(0), 1: lambda: exponential(0), 4: lambda: rstd(1), 5: lambda: exponential(1),
                          len(between) - 1: store_diagonals}

                step("null key's norm", lambda: nc.scalar.activation(nk[:, 2:3], nk[:, 1:2], ACT.Ln, scale=NORM_SCALE))
                step("null key's norm", lambda: nc.scalar.activation(nk[:, 3:4], nk[:, 2:3], ACT.Exp, scale=-0.5, bias=root_col[:, 0:1]))
                for what, k in order:
                    if what == "phase":
                        if k in phases:
                            phases[k]()
                        continue
                    high_part(k)
                    if k == sum(between) + 1:
                        act.wait_ge(diag_stored, 32)
                        for c in range(4):
                            act.dma_start(bias[1][:, 4 * c:4 * c + 4, :],
                                          bass.AP(diagonals.tensor, 4 * c * 2 * S, [[1, P], [2 * S, 4], [1, S]])
                                          ).then_inc(diag_loaded[c], 16)
                for c in range(4):
                    act.wait_ge(flipped, c + 1)
                    nc.scalar.copy(bias[1][:, 4 * c:4 * c + 4, :], psum[:, 3 + c, :].rearrange("p (h s) -> p h s", h=4))

            @block.gpsimd
            def _(pool):
                nc.gpsimd.iota(pos[:, :], pattern=[[0, 1]], base=S - 1, channel_multiplier=-1,
                               allow_small_or_imprecise_dtypes=True).then_inc(pos_done, 1)
                nc.gpsimd.memset(neg_tile[:, :], NEG).then_inc(neg_tile_done, 1)
                nc.gpsimd.memset(ident[:, :], 0.0).then_inc(ident_zero, 1)
                pool.wait_ge(ident_zero, 1)
                nc.gpsimd.affine_select(out=ident[:, :], in_=ident[:, :], compare_op=ALU.not_equal, fill=1.0, base=0,
                                        pattern=[[-1, P]], channel_multiplier=1).then_inc(ident_done, 1)
                nc.gpsimd.memset(flip[:, :], 0.0).then_inc(ident_zero, 1)
                pool.wait_ge(ident_zero, 2)
                nc.gpsimd.affine_select(out=flip[:, :], in_=flip[:, :], compare_op=ALU.not_equal, fill=1.0, base=1 - S,
                                        pattern=[[1, P]], channel_multiplier=1).then_inc(flip_done, 1)
                for i in range(IN):
                    n = pieces[i][1]
                    pool.wait_ge(null_key_done, n + 1)
                    wait_piece(pool, i)
                    if i >= 2:
                        pool.wait_ge(w0_done, i - 1)
                    nc.gpsimd.tensor_tensor(prod[:, i % 2, :].rearrange("p (h d) -> p h d", d=DH),
                                            split_piece(i)[0][:, 0:INNER].rearrange("p (h d) -> p h d", d=DH),
                                            null_key[n][:, :].unsqueeze(1).to_broadcast([P, H, DH]),
                                            ALU.mult).then_inc(w0_multiplied, 1)
                pool.wait_ge(rest_loaded, 16 * len(rest_loads))
                nc.gpsimd.affine_select(out=bias[0][:, :, :], in_=bias[0][:, :, :], compare_op=ALU.is_ge, fill=NEG, base=0,
                                        pattern=[[0, H], [-1, S]], channel_multiplier=1).then_inc(causal_done, 1)
                for i, engine in enumerate(lo_engine):
                    if engine == "pool":
                        _, src, hi, lo = split_piece(i)
                        pool.wait_ge(hi_done, i + 1)
                        nc.gpsimd.tensor_tensor(lo, src, hi.bitcast(F32), ALU.subtract).then_inc(lo_done["pool"], 1)
                pool.wait_ge(causal_done, 1)

            @block.tensor
            def _(pe):
                pe.wait_ge(ident_done, 1)

                def transposed_h(layer):
                    pe.wait_ge(dve_step, marks[f"silu {layer}"])
                    for c in range(KC):
                        t = nc.tensor.transpose(psum[:, 0, c * P:(c + 1) * P], h[:, c * P:(c + 1) * P], ident[:, :])
                    t.then_inc(pe_step, 1)

                transposed_h(0)
                pe.wait_ge(dve_step, marks["silu^T 0"])
                pe.wait_ge(w1_loaded, 16 * len(w1_loads))
                for c in range(KC):
                    m = nc.tensor.matmul(psum[:, 1, :], h_t[:, c * P:(c + 1) * P], w1[:, c, :], start=(c == 0), stop=(c == KC - 1))
                m.then_inc(pe_step, 1)
                transposed_h(1)
                pe.wait_ge(dve_step, marks["silu^T 1"])
                for c in range(KC):
                    m = nc.tensor.matmul(psum[:, 1, 0:H], h_t[:, c * P:(c + 1) * P], w2[:, c, :], start=(c == 0), stop=(c == KC - 1))
                m.then_inc(pe_step, 1)
                pe.wait_ge(dve_step, marks["diagonals"])
                nc.tensor.transpose(psum[0:H, 2, 0:S], diag_sb[:, :], ident[:, :]).then_inc(pe_step, 1)
                pe.wait_ge(flip_done, 1)
                for c in range(4):
                    pe.wait_ge(diag_loaded[c], 16)
                    nc.tensor.matmul(psum[:, 3 + c, :], flip[:, :], bias[1][:, 4 * c:4 * c + 4, :].rearrange("p h s -> p (h s)"),
                                     start=True, stop=True).then_inc(flipped, 1)


_COMMON = ["x", "fside_16xSxS_0", "cond_64", "mask_BxS_bk0", "mask_BxS_bf1"]
_L0 = {"g_in": "g_in", "null_bias": "null_attn_bias", "Wq": "Wq", "Wkv": "Wkv", "Wo": "Wo", "g_out": "g_out"}
_L1 = {"g_in": "g_norm", "null_bias": "null_attn_bias", "Wq": "Wq", "Wkv": "Wkv", "Wo": "Wout", "g_out": "g_out",
       "q_scale": "q_scale", "k_scale": "k_scale", "w0": "w0", "b0": "b0", "g0": "g0", "w1": "w1", "b1": "b1", "g1": "g1",
       "w2": "w2", "b2": "b2"}


def kernel(**inputs):
    import numpy as _np
    import concourse.bacc as _bacc
    from concourse import mybir as _mybir
    from concourse.bass_utils import run_bass_kernel_spmd as _run

    nc = _bacc.Bacc("TRN2", target_bir_lowering=False, num_devices=1,
                    dynamic_dma_scratch_size=1024)
    arrays = {}

    def give(name):
        a = _np.ascontiguousarray(inputs[name])
        if name == "L1_cond_w0":
            a = a.reshape(-1)
        arrays[f"in_{name}_dram"] = a
        return nc.dram_tensor(f"in_{name}_dram", a.shape, _mybir.dt.from_np(a.dtype), kind="ExternalInput").ap()

    x, bias0, null_kv, keep0, keep1 = (give(n) for n in _COMMON)
    L0 = {k: give("L0_cond_" + n) for k, n in _L0.items()}
    L1 = {k: give("L1_cond_" + n) for k, n in _L1.items()}
    out = nc.dram_tensor("out_0_dram", inputs["x"].shape, F32, kind="ExternalOutput").ap()
    build(nc, x, bias0, null_kv, keep0, keep1, L0, L1, out)
    r = _run(nc, [arrays], core_ids=[0])
    return r.results[0]["out_0_dram"]
```
